# Optimizing a Trainium2 kernel written in Bass

```python
import numpy as np
import jax
import jax.numpy as jnp

def _softmax(x, axis=-1):
    return jax.nn.softmax(x, axis=axis)

def _gelu(x):
    return jax.nn.gelu(x, approximate=True)

def _silu(x):
    return jax.nn.silu(x)

def _sigmoid(x):
    return jax.nn.sigmoid(x)

def _layernorm(x, axis=-1, eps=1e-05):
    m = jnp.mean(x, axis=axis, keepdims=True)
    v = jnp.var(x, axis=axis, keepdims=True)
    return (x - m) / jnp.sqrt(v + eps)

def _scatter_add(tgt, idx, src, axis=0):
    return tgt.at[idx].add(src)

def _segment_sum(src, seg, n):
    return jax.ops.segment_sum(src, seg, n)
kernel_name = 'mk_cond_seq_d4_seqx_r8_5e3d57'

def setup_inputs(seed: int=0):
    np.random.seed(seed)
    _w = jnp.asarray

    def _rec_inputs():
        import jax
        import jax.numpy as jnp
        _rk = jax.random.key(seed)
        x = -0.000125 + 0.9999 * jax.random.normal(jax.random.fold_in(_rk, 1), (32, 32, 128), jnp.float32)
        _lenS = 32 - jax.random.randint(jax.random.fold_in(_rk, 7), (32,), 0, max(1, 32 // 4) + 1, jnp.int32)
        _lenS2 = 32 - jax.random.randint(jax.random.fold_in(_rk, 8), (32,), 0, max(1, 32 // 4) + 1, jnp.int32)
        itok_B_0_15 = jax.random.randint(jax.random.fold_in(_rk, 11), (32,), 0, 16, jnp.int32)
        itok_B_0_7 = jax.random.randint(jax.random.fold_in(_rk, 12), (32,), 0, 8, jnp.int32)
        itok_B_0_2 = jax.random.randint(jax.random.fold_in(_rk, 13), (32,), 0, 3, jnp.int32)
        condB_theta = jax.random.uniform(jax.random.fold_in(_rk, 14), (32,), jnp.float32, 0.0, 0.983423)
        condB_phi = jax.random.uniform(jax.random.fold_in(_rk, 15), (32,), jnp.float32, 0.0, 0.961312)
        return (x, itok_B_0_15, itok_B_0_7, itok_B_0_2, condB_theta, condB_phi)
    x, itok_B_0_15, itok_B_0_7, itok_B_0_2, condB_theta, condB_phi = _rec_inputs()

    def _L0_cond_setup():
        import jax, jax.numpy as jnp
        import numpy as np
        B, S, D = (32, 128, 128)
        A = 32
        E = 16
        LN_EPS = 1e-05
        key = jax.random.key(seed)
        ks = jax.random.split(key, 10)
        s = lambda fan_in: 1.0 / np.sqrt(fan_in)
        return {'hidden_states': jax.random.normal(ks[0], (B, S, D), dtype=jnp.float32), 'domain_id': jax.random.randint(ks[1], (B,), 0, E, dtype=jnp.int64), 'down_W': jax.random.uniform(ks[2], (A, D), jnp.float32, -s(D), s(D)), 'down_b': jax.random.uniform(ks[3], (A,), jnp.float32, -s(D), s(D)), 'up_W': jax.random.uniform(ks[4], (D, A), jnp.float32, -s(A), s(A)), 'up_b': jax.random.uniform(ks[5], (D,), jnp.float32, -s(A), s(A)), 'expert_W': jax.random.uniform(ks[6], (E, A, A), jnp.float32, -s(A), s(A)), 'expert_b': jax.random.uniform(ks[7], (E, A), jnp.float32, -s(A), s(A)), 'domain_emb': jax.random.normal(ks[8], (E, A), dtype=jnp.float32), 'ln_gamma': jnp.ones((D,), jnp.float32), 'ln_beta': jnp.zeros((D,), jnp.float32)}
    _L0_cond_all = _L0_cond_setup()
    _L0_cond_in = {k: v for k, v in _L0_cond_all.items() if k in ('down_W', 'down_b', 'up_W', 'up_b', 'expert_W', 'expert_b', 'domain_emb', 'ln_gamma', 'ln_beta')}
    del _L0_cond_all

    def _L1_cond_setup():
        import jax, jax.numpy as jnp
        import numpy as np
        E, H, I = (8, 128, 512)
        B, S = (4, 128)
        LN_EPS = 1e-12
        key = jax.random.key(seed)
        ks = jax.random.split(key, 8)
        x = jax.random.normal(ks[0], (B, S, H), dtype=jnp.float32)
        expert_idx = jax.random.randint(ks[1], (B,), 0, E, dtype=jnp.int64)
        Wi = jax.random.normal(ks[2], (E, H, I), dtype=jnp.float32) * 0.02
        bi = jnp.zeros((E, I), dtype=jnp.float32)
        Wo = jax.random.normal(ks[3], (E, I, H), dtype=jnp.float32) * 0.02
        bo = jnp.zeros((E, H), dtype=jnp.float32)
        gamma = jnp.ones((E, H), dtype=jnp.float32)
        beta = jnp.zeros((E, H), dtype=jnp.float32)
        return {'input_tensor': x, 'expert_idx': expert_idx, 'Wi': Wi, 'bi': bi, 'Wo': Wo, 'bo': bo, 'gamma': gamma, 'beta': beta}
    _L1_cond_all = _L1_cond_setup()
    _L1_cond_in = {k: v for k, v in _L1_cond_all.items() if k in ('Wi', 'bi', 'Wo', 'bo', 'gamma', 'beta')}
    del _L1_cond_all

    def _L2_cond_setup():
        import jax, jax.numpy as jnp
        import numpy as np
        H = 128
        EPS = 1e-05

        def _gelu(x):
            return jax.nn.gelu(x, approximate=False)
        key = jax.random.key(seed)
        ks = jax.random.split(key, 16)
        s = 1.0 / np.sqrt(H)
        inp = {'x': jax.random.normal(ks[0], (64, 128, H), dtype=jnp.float32), 'condition': jax.random.randint(ks[1], (64,), 0, 3), 'w1_nr': jax.random.normal(ks[2], (H, H), dtype=jnp.float32) * s, 'b1_nr': jnp.zeros((H,), dtype=jnp.float32), 'w2_nr': jax.random.normal(ks[3], (H, H), dtype=jnp.float32) * s, 'b2_nr': jnp.zeros((H,), dtype=jnp.float32), 'w1_tsr': jax.random.normal(ks[4], (H, H), dtype=jnp.float32) * s, 'b1_tsr': jnp.zeros((H,), dtype=jnp.float32), 'w2_tsr': jax.random.normal(ks[5], (H, H), dtype=jnp.float32) * s, 'b2_tsr': jnp.zeros((H,), dtype=jnp.float32), 'w1_sr': jax.random.normal(ks[6], (H, 2 * H), dtype=jnp.float32) * s, 'b1_sr': jnp.zeros((2 * H,), dtype=jnp.float32), 'w2_sr': jax.random.normal(ks[7], (2 * H, H), dtype=jnp.float32) * (1.0 / np.sqrt(2 * H)), 'b2_sr': jnp.zeros((H,), dtype=jnp.float32), 'w3_sr': jax.random.normal(ks[8], (H, H), dtype=jnp.float32) * s, 'b3_sr': jnp.zeros((H,), dtype=jnp.float32), 'gamma': jnp.ones((H,), dtype=jnp.float32), 'beta': jnp.zeros((H,), dtype=jnp.float32)}
        return inp
    _L2_cond_all = _L2_cond_setup()
    _L2_cond_in = {k: v for k, v in _L2_cond_all.items() if k in ('w1_nr', 'b1_nr', 'w2_nr', 'b2_nr', 'w1_tsr', 'b1_tsr', 'w2_tsr', 'b2_tsr', 'w1_sr', 'b1_sr', 'w2_sr', 'b2_sr', 'w3_sr', 'b3_sr', 'gamma', 'beta')}
    del _L2_cond_all

    def _L3_cond_setup():
        import jax, jax.numpy as jnp
        import numpy as np
        key = jax.random.key(seed)
        k1, k2, k3 = jax.random.split(key, 3)
        B, N, D = (16, 512, 128)
        embeddings = jax.random.normal(k1, (B, N, D), dtype=jnp.float32)
        theta = jax.random.uniform(k2, (B,), dtype=jnp.float32)
        phi = jax.random.uniform(k3, (B,), dtype=jnp.float32)
        return {'embeddings': embeddings, 'theta': theta, 'phi': phi}
    _L3_cond_all = _L3_cond_setup()
    _L3_cond_in = {k: v for k, v in _L3_cond_all.items() if k in ()}
    del _L3_cond_all
    return {'x': x, 'itok_B_0_15': itok_B_0_15, 'itok_B_0_7': itok_B_0_7, 'itok_B_0_2': itok_B_0_2, 'condB_theta': condB_theta, 'condB_phi': condB_phi, 'L0_cond_down_W': _L0_cond_in['down_W'], 'L0_cond_down_b': _L0_cond_in['down_b'], 'L0_cond_up_W': _L0_cond_in['up_W'], 'L0_cond_up_b': _L0_cond_in['up_b'], 'L0_cond_expert_W': _L0_cond_in['expert_W'], 'L0_cond_expert_b': _L0_cond_in['expert_b'], 'L0_cond_domain_emb': _L0_cond_in['domain_emb'], 'L0_cond_ln_gamma': _L0_cond_in['ln_gamma'], 'L0_cond_ln_beta': _L0_cond_in['ln_beta'], 'L1_cond_Wi': _L1_cond_in['Wi'], 'L1_cond_bi': _L1_cond_in['bi'], 'L1_cond_Wo': _L1_cond_in['Wo'], 'L1_cond_bo': _L1_cond_in['bo'], 'L1_cond_gamma': _L1_cond_in['gamma'], 'L1_cond_beta': _L1_cond_in['beta'], 'L2_cond_w1_nr': _L2_cond_in['w1_nr'], 'L2_cond_b1_nr': _L2_cond_in['b1_nr'], 'L2_cond_w2_nr': _L2_cond_in['w2_nr'], 'L2_cond_b2_nr': _L2_cond_in['b2_nr'], 'L2_cond_w1_tsr': _L2_cond_in['w1_tsr'], 'L2_cond_b1_tsr': _L2_cond_in['b1_tsr'], 'L2_cond_w2_tsr': _L2_cond_in['w2_tsr'], 'L2_cond_b2_tsr': _L2_cond_in['b2_tsr'], 'L2_cond_w1_sr': _L2_cond_in['w1_sr'], 'L2_cond_b1_sr': _L2_cond_in['b1_sr'], 'L2_cond_w2_sr': _L2_cond_in['w2_sr'], 'L2_cond_b2_sr': _L2_cond_in['b2_sr'], 'L2_cond_w3_sr': _L2_cond_in['w3_sr'], 'L2_cond_b3_sr': _L2_cond_in['b3_sr'], 'L2_cond_gamma': _L2_cond_in['gamma'], 'L2_cond_beta': _L2_cond_in['beta']}

def reference(x, itok_B_0_15, itok_B_0_7, itok_B_0_2, condB_theta, condB_phi, L0_cond_down_W, L0_cond_down_b, L0_cond_up_W, L0_cond_up_b, L0_cond_expert_W, L0_cond_expert_b, L0_cond_domain_emb, L0_cond_ln_gamma, L0_cond_ln_beta, L1_cond_Wi, L1_cond_bi, L1_cond_Wo, L1_cond_bo, L1_cond_gamma, L1_cond_beta, L2_cond_w1_nr, L2_cond_b1_nr, L2_cond_w2_nr, L2_cond_b2_nr, L2_cond_w1_tsr, L2_cond_b1_tsr, L2_cond_w2_tsr, L2_cond_b2_tsr, L2_cond_w1_sr, L2_cond_b1_sr, L2_cond_w2_sr, L2_cond_b2_sr, L2_cond_w3_sr, L2_cond_b3_sr, L2_cond_gamma, L2_cond_beta):
    import jax
    import jax.numpy as jnp

    def _L0_cond_ref(hidden_states, domain_id, down_W, down_b, up_W, up_b, expert_W, expert_b, domain_emb, ln_gamma, ln_beta):
        import jax, jax.numpy as jnp
        import numpy as np
        B, S, D = (32, 128, 128)
        A = 32
        E = 16
        LN_EPS = 1e-05
        residual = hidden_states
        hidden = jnp.einsum('bsd,ad->bsa', hidden_states, down_W) + down_b
        hidden = jax.nn.gelu(hidden, approximate=False)
        valid = (domain_id >= 0) & (domain_id < E)
        idx = jnp.clip(domain_id, 0, E - 1)
        Wsel = expert_W[idx]
        bsel = expert_b[idx]
        expert_out = jnp.einsum('bsa,boa->bso', hidden, Wsel) + bsel[:, None, :]
        domain_output = jnp.where(valid[:, None, None], expert_out, hidden)
        hidden = domain_output + domain_emb[idx][:, None, :]
        hidden = jnp.einsum('bsa,da->bsd', hidden, up_W) + up_b
        x = hidden + residual
        mu = jnp.mean(x, axis=-1, keepdims=True)
        var = jnp.mean(jnp.square(x - mu), axis=-1, keepdims=True)
        return (x - mu) * jax.lax.rsqrt(var + LN_EPS) * ln_gamma + ln_beta

    def _L1_cond_ref(input_tensor, expert_idx, Wi, bi, Wo, bo, gamma, beta):
        import jax, jax.numpy as jnp
        import numpy as np
        E, H, I = (8, 128, 512)
        B, S = (4, 128)
        LN_EPS = 1e-12
        Wi_b = Wi[expert_idx]
        bi_b = bi[expert_idx]
        Wo_b = Wo[expert_idx]
        bo_b = bo[expert_idx]
        g_b = gamma[expert_idx]
        be_b = beta[expert_idx]
        h = jax.nn.gelu(jnp.einsum('bsh,bhi->bsi', input_tensor, Wi_b) + bi_b[:, None, :], approximate=False)
        o = jnp.einsum('bsi,bih->bsh', h, Wo_b) + bo_b[:, None, :]
        r = o + input_tensor
        mu = jnp.mean(r, axis=-1, keepdims=True)
        var = jnp.mean(jnp.square(r - mu), axis=-1, keepdims=True)
        y = (r - mu) * jax.lax.rsqrt(var + LN_EPS)
        return y * g_b[:, None, :] + be_b[:, None, :]

    def _L2_cond_ref(x, condition, w1_nr, b1_nr, w2_nr, b2_nr, w1_tsr, b1_tsr, w2_tsr, b2_tsr, w1_sr, b1_sr, w2_sr, b2_sr, w3_sr, b3_sr, gamma, beta):
        import jax, jax.numpy as jnp
        import numpy as np
        H = 128
        EPS = 1e-05

        def _gelu(x):
            return jax.nn.gelu(x, approximate=False)
        out_nr = _gelu(jnp.einsum('bth,hk->btk', x, w1_nr) + b1_nr)
        out_nr = jnp.einsum('bth,hk->btk', out_nr, w2_nr) + b2_nr
        out_tsr = _gelu(jnp.einsum('bth,hk->btk', x, w1_tsr) + b1_tsr)
        out_tsr = jnp.einsum('bth,hk->btk', out_tsr, w2_tsr) + b2_tsr
        h = _gelu(jnp.einsum('bth,hk->btk', x, w1_sr) + b1_sr)
        h = _gelu(jnp.einsum('bth,hk->btk', h, w2_sr) + b2_sr)
        out_sr = jnp.einsum('bth,hk->btk', h, w3_sr) + b3_sr
        c = condition[:, None, None]
        out = jnp.where(c == 0, out_nr, jnp.where(c == 1, out_tsr, jnp.where(c == 2, out_sr, jnp.zeros_like(x))))
        y = x + out
        mu = jnp.mean(y, axis=-1, keepdims=True)
        var = jnp.mean((y - mu) ** 2, axis=-1, keepdims=True)
        return (y - mu) * jax.lax.rsqrt(var + EPS) * gamma + beta

    def _L3_cond_ref(embeddings, theta, phi):
        import jax, jax.numpy as jnp
        import numpy as np
        B, N, D = embeddings.shape
        e = embeddings.reshape(B, N, D // 4, 4)
        ct = jnp.cos(theta)[:, None, None]
        st = jnp.sin(theta)[:, None, None]
        cp = jnp.cos(phi)[:, None, None]
        sp = jnp.sin(phi)[:, None, None]
        x0, x1, x2, x3 = (e[..., 0], e[..., 1], e[..., 2], e[..., 3])
        out = jnp.stack([x0 * ct + x1 * st, -x0 * st + x1 * ct, x2 * cp + x3 * sp, -x2 * sp + x3 * cp], axis=-1)
        return out.reshape(B, N, D)
    x = _L0_cond_ref(x, itok_B_0_15, L0_cond_down_W, L0_cond_down_b, L0_cond_up_W, L0_cond_up_b, L0_cond_expert_W, L0_cond_expert_b, L0_cond_domain_emb, L0_cond_ln_gamma, L0_cond_ln_beta)
    x = _L1_cond_ref(x, itok_B_0_7, L1_cond_Wi, L1_cond_bi, L1_cond_Wo, L1_cond_bo, L1_cond_gamma, L1_cond_beta)
    x = _L2_cond_ref(x, itok_B_0_2, L2_cond_w1_nr, L2_cond_b1_nr, L2_cond_w2_nr, L2_cond_b2_nr, L2_cond_w1_tsr, L2_cond_b1_tsr, L2_cond_w2_tsr, L2_cond_b2_tsr, L2_cond_w1_sr, L2_cond_b1_sr, L2_cond_w2_sr, L2_cond_b2_sr, L2_cond_w3_sr, L2_cond_b3_sr, L2_cond_gamma, L2_cond_beta)
    x = _L3_cond_ref(x, condB_theta, condB_phi)
    return x

_drawn_inputs = setup_inputs


def setup_inputs(seed=0):
    import zlib

    import numpy as np

    out = dict(_drawn_inputs(seed))
    spreads = {'L0_cond_ln_gamma': (1.0, 0.2),
     'L0_cond_ln_beta': (0.0, 0.1),
     'L1_cond_bi': (0.0, 0.358),
     'L1_cond_bo': (0.0, 0.1),
     'L1_cond_gamma': (1.0, 0.2),
     'L1_cond_beta': (0.0, 0.1),
     'L2_cond_b1_nr': (0.0, 0.287),
     'L2_cond_b2_nr': (0.0, 0.1),
     'L2_cond_b1_tsr': (0.0, 0.1),
     'L2_cond_b2_tsr': (0.0, 0.1),
     'L2_cond_b1_sr': (0.0, 0.35),
     'L2_cond_b2_sr': (0.0, 0.1),
     'L2_cond_b3_sr': (0.0, 0.1),
     'L2_cond_gamma': (1.0, 0.2),
     'L2_cond_beta': (0.0, 0.1)}
    factors = {'L0_cond_down_b': 5.93}
    for name, (base, spread) in spreads.items():
        noise = np.random.default_rng([zlib.crc32(name.encode()), seed]).standard_normal(out[name].shape)
        drawn = base * np.exp(spread * noise) if base else spread * noise
        out[name] = jnp.asarray(drawn.astype(out[name].dtype))
    for name, factor in factors.items():
        out[name] = (out[name] * factor).astype(out[name].dtype)
    return out
```

```python
import concourse.bass as bass
from concourse import mybir
from contextlib import ExitStack

fp32 = mybir.dt.float32
bf16 = mybir.dt.bfloat16
i32 = mybir.dt.int32
ACT = mybir.ActivationFunctionType
ALU = mybir.AluOpType
AX = mybir.AxisListType

P = 128
B, S, D = 32, 32, 128
NT = B * S // P
BT = P // S
HALF = NT // 2
HC = HALF * P
A, E0 = 32, 16
E1, I1 = 8, 512
NC1 = I1 // P
NW = (B + (BT - 1) * E1) // BT
PADDED = (B + BT) * S
HALF_PI = 1.5707963267948966

R_BI, R_BO, R_G1, R_BE1 = 0, 32, 40, 48
R_G0, R_BE0, R_NR, R_TSR, R_SR, R_SR2, R_DB = 56, 57, 58, 59, 60, 62, 63
NR = 64
T_ID, T_COS, T_SIN, T_COND, NTAB = 0, 1, 5, 9, 10


def conditional_layers(nc, x, idx_domain, idx_expert, idx_cond, theta, phi,
                       down_W, down_b, up_W, up_b, expert_W, expert_b, domain_emb, g0, be0,
                       Wi, bi, Wo, bo, g1, be1,
                       w1_nr, b1_nr, w2_nr, b2_nr, w1_tsr, b1_tsr, w2_tsr, b2_tsr,
                       w1_sr, b1_sr, w2_sr, b2_sr, w3_sr, b3_sr, g2, be2, out):
    ctx = ExitStack()
    with ctx:
        def sb(name, shape, dt=fp32):
            return ctx.enter_context(nc.sbuf_tensor(name, shape, dt))

        def sem(name):
            return ctx.enter_context(nc.semaphore(name))

        x_tok = sb("x_tok", [P, NT, D])
        xT = sb("xT", [P, NT * P])
        x1T = sb("x1T", [P, PADDED])
        x2T = sb("x2T", [P, PADDED])
        ident = sb("ident", [P, P])
        vec_rows = sb("vec_rows", [NR, P])
        vecT = sb("vecT", [P, NR])
        down4 = sb("down4", [P, D])
        down4T = sb("down4T", [P, P])
        up4 = sb("up4", [P, BT, A])
        up4T = sb("up4T", [P, D])
        hid_bd = sb("hid_bd", [P, NT, P])
        wg = sb("wg", [P, NT, A])
        wg_bd = sb("wg_bd", [P, NT, BT, A])
        G = sb("G", [P, NT, D])
        eb_rows = sb("eb_rows", [B, A])
        emb_rows = sb("emb_rows", [B, A])
        bsum = sb("bsum", [B, A])
        bsumT = sb("bsumT", [A, B])
        cb = sb("cb", [B, D])
        up_b_rows = sb("up_b_rows", [B, D])
        batch_of = sb("batch_of", [B, NT * P])
        dom_i = sb("dom_i", [P, B], i32)
        dom_f = sb("dom_f", [P, B])
        dom_t = sb("dom_t", [P, NT, BT])
        dom_p = sb("dom_p", [P, NT])
        dom_c = sb("dom_c", [P, NT])
        valid_p = sb("valid_p", [P, NT])
        valid_2 = sb("valid_2", [P, NT])
        widx_f = sb("widx_f", [P, NT])
        widx = sb("widx", [P, NT], i32)
        domcol_i = sb("domcol_i", [B, 1], i32)
        domcol = sb("domcol", [B, 4])
        domidx = sb("domidx", [B, 1], i32)
        quad = sb("quad", [P, BT])
        quad_o = sb("quad_o", [P, BT])
        eye32 = sb("eye32", [P, A])
        eye_inv = sb("eye_inv", [P, NT, A])
        p_int = sb("p_int", [P, 2], i32)
        p_mod = sb("p_mod", [P, 1])
        exp_i = sb("exp_i", [P, B], i32)
        exp_f = sb("exp_f", [P, B])
        keys = sb("keys", [B, B])
        expcol_i = sb("expcol_i", [B, 1], i32)
        keycol = sb("keycol", [B, 2])
        before = sb("before", [B, B])
        rank = sb("rank", [B, B])
        rankT = sb("rankT", [B, B])
        rank_cols = sb("rank_cols", [1, B], i32)
        iota_b = sb("iota_b", [B, B])
        iota_p = sb("iota_p", [B, 1])
        slot_of = sb("slot_of", [B, NT * P])
        perm = sb("perm", [B, NT * P])
        perm_h = sb("perm_h", [B, NT * P], bf16)
        table = sb("table", [B, NTAB])
        angles = sb("angles", [B, 8])
        tp = sb("tp", [B, 2])
        tok_tab = sb("tok_tab", [P, NT, NTAB])
        tok_f = sb("tok_f", [P, NT])
        tok_idx = sb("tok_idx", [P, NT], i32)
        cond_i = sb("cond_i", [B, 1], i32)
        cond_rep = sb("cond_rep", [B, P], bf16)
        cond_row = sb("cond_row", [P, NT * P])
        ewi = sb("ewi", [1, NW])
        c_lt = sb("c_lt", [1, E1 + 1, B])
        s_cum = sb("s_cum", [1, E1 + 1])
        n_e = sb("n_e", [1, E1])
        c_nw = sb("c_nw", [1, E1, E1])
        nw_e = sb("nw_e", [1, E1])
        tri = sb("tri", [1, E1, E1])
        cw = sb("cw", [1, E1])
        cwx = sb("cwx", [1, E1])
        base = sb("base", [1, E1])
        c_w = sb("c_w", [1, NW, E1])
        e_w = sb("e_w", [1, NW])
        s_w = sb("s_w", [1, NW])
        v_w = sb("v_w", [1, NW])
        win = sb("win", [1, 2, NW], i32)
        iota_r = sb("iota_r", [1, B])
        r_sb = sb("r_sb", [P, 2, HALF, D])
        stats = sb("stats", [P, 2, HALF, 6])
        mv = sb("mv", [P, 2, HALF, 2])
        rstd = sb("rstd", [P, 2, HALF])
        vpe = sb("vpe", [P, 2, HALF])
        mhalf = sb("mhalf", [P, HALF])
        z0 = sb("z0", [P, NT, D])
        wi_st = sb("wi_st", [P, 3, I1])
        wo = sb("wo", [P, E1, NC1, D])
        hT = sb("hT", [P, 2, I1])
        xrT = sb("xrT", [P, 2, P])
        z1 = sb("z1", [P, 2, D])
        st1 = sb("st1", [P, 2, 6])
        mv1 = sb("mv1", [P, 2, 2])
        vpe1 = sb("vpe1", [P, 2, 1])
        rstd1 = sb("rstd1", [P, 2, 1])
        w1 = sb("w1", [P, 4, P])
        w2s = sb("w2s", [P, 2, P])
        w_last = sb("w_last", [P, 3, P])
        h2 = sb("h2", [P, 2, 4, HC])
        h3 = sb("h3", [P, 2, HC])
        b_last = sb("b_last", [P, 3, D])
        g2r = sb("g2r", [P, D])
        be2r = sb("be2r", [P, D])
        c_last = sb("c_last", [P, NT, D])
        rot_a = sb("rot_a", [P, NT, D])
        rot_b = sb("rot_b", [P, NT, D])
        rot_c = sb("rot_c", [P, NT, D])
        rot_t = sb("rot_t", [P, NT, D])
        is_c = sb("is_c", [P, 3, NT])
        z2 = sb("z2", [P, NT, D])
        y_a = sb("y_a", [P, NT, D])
        y_b = sb("y_b", [P, NT, D])
        y = sb("y", [P, NT, D])

        bank = [ctx.enter_context(nc.psum_tensor(f"bank{i}", [P, 512], fp32)) for i in range(8)]

        ld_idx = sem("ld_idx")
        ld_x = [sem(f"ld_x{i}") for i in range(2)]
        ld_vec = sem("ld_vec")
        ld_du = sem("ld_du")
        ld_ang = sem("ld_ang")
        ld_wg = sem("ld_wg")
        ld_eb = sem("ld_eb")
        ld_upb = sem("ld_upb")
        ld_wo = sem("ld_wo")
        ld_l2 = sem("ld_l2")
        ld_rows = sem("ld_rows")
        ld_wi = [sem(f"ld_wi{i}") for i in range(3)]
        stored = sem("stored")
        pool_c = sem("pool_c")
        consts = sem("consts")
        widx_ready = sem("widx_ready")
        ranked = sem("ranked")
        perm_ready = sem("perm_ready")
        table_ready = sem("table_ready")
        cond_rep_ready = sem("cond_rep_ready")
        angles_ready = sem("angles_ready")
        win_ready = sem("win_ready")
        small_T = sem("small_T")
        small_copied = sem("small_copied")
        xT_psum = sem("xT_psum")
        xT_ready = sem("xT_ready")
        up4_ready = sem("up4_ready")
        hid_psum = sem("hid_psum")
        hid_ready = sem("hid_ready")
        bd_ready = sem("bd_ready")
        g_psum = sem("g_psum")
        g_ready = sem("g_ready")
        bsumT_ready = sem("bsumT_ready")
        cb_psum = sem("cb_psum")
        cb_ready = sem("cb_ready")
        tab_psum = sem("tab_psum")
        tab_ready = sem("tab_ready")
        cond_psum = sem("cond_psum")
        cond_ready = sem("cond_ready")
        o0_psum = sem("o0_psum")
        mv_ready = sem("mv_ready")
        rstd_ready = sem("rstd_ready")
        z0_ready = sem("z0_ready")
        z0T_psum = sem("z0T_psum")
        x1_ready = sem("x1_ready")
        up_done = sem("up_done")
        gelu_done = sem("gelu_done")
        xr_ready = sem("xr_ready")
        down_done = sem("down_done")
        mv1_ready = sem("mv1_ready")
        rstd1_ready = sem("rstd1_ready")
        z1_ready = sem("z1_ready")
        z1T_done = sem("z1T_done")
        x2_done = sem("x2_done")
        vpe_s = sem("vpe_s")
        l2_psum = sem("l2_psum")
        l2_gelu = sem("l2_gelu")
        masked = sem("masked")
        last_psum = sem("last_psum")
        clast_ready = sem("clast_ready")
        rot_ready = sem("rot_ready")
        z2_ready = sem("z2_ready")
        yb_ready = sem("yb_ready")
        y_ready = sem("y_ready")
        dstep = sem("dstep")
        pstep = sem("pstep")
        astep = sem("astep")

        block = ctx.enter_context(nc.Block())

        def row(v, n=None):
            return v.rearrange("(a b) -> a b", a=1)

        def col(v):
            return v.rearrange("(a b) -> a b", b=1)

        def everywhere(v, parts):
            return row(v).to_broadcast([parts, v.shape[0]])

        def win_value(eng, which, w, top):
            return eng.value_load(win[0:1, which, bass.ds(w, 1)], min_val=0, max_val=top)

        x_view = x.rearrange("(t r) s d -> (r s) t d", r=BT)
        out_rows = out.rearrange("b s d -> (b s) d")

        @block.sync
        def _(sp):
            sp.dma_start(dom_i[:, :], everywhere(idx_domain, P)).then_inc(ld_idx, 16)
            sp.dma_start(exp_i[:, :], everywhere(idx_expert, P)).then_inc(ld_idx, 16)
            for h in range(2):
                sp.dma_start(x_tok[:, h * HALF:(h + 1) * HALF, :],
                             x_view[:, h * HALF:(h + 1) * HALF, :]).then_inc(ld_x[h], 16)
            sp.dma_start(domcol_i[:, :], col(idx_domain)).then_inc(ld_idx, 16)
            sp.dma_start(expcol_i[:, :], col(idx_expert)).then_inc(ld_idx, 16)
            sp.dma_start(cond_i[:, :], col(idx_cond)).then_inc(ld_idx, 16)
            for i, v in enumerate((theta, phi)):
                sp.dma_start(tp[:, i:i + 1], col(v)).then_inc(ld_ang, 16)
            sp.wait_ge(win_ready, 1)

            def load_wi(w, slot):
                e = win_value(sp, 1, w, E1 - 1)
                sp.dma_start(wi_st[:, slot, :],
                             Wi.rearrange("e h i -> (e h) i")[bass.ds(e * P, P), :]).then_inc(ld_wi[slot], 16)

            load_wi(0, 0)
            for h in range(2):
                sp.dma_start(wo[:, h * E1 // 2:(h + 1) * E1 // 2, :, :],
                             Wo[h * E1 // 2:(h + 1) * E1 // 2].rearrange("e (c i) h -> i e c h", i=P)
                             ).then_inc(ld_wo, 16)
            load_wi(1, 1)
            load_wi(2, 2)
            for w in range(3, NW):
                sp.wait_ge(up_done, w - 2)
                load_wi(w, w % 3)
            sp.wait_ge(stored, 16 * NT)

        @block.tensor
        def _(pe):
            T = nc.tensor
            pe.wait_ge(consts, 1)
            for h in range(2):
                pe.wait_ge(ld_x[h], 16)
                for k in range(HALF):
                    last = T.transpose(bank[h][:, k * P:(k + 1) * P], x_tok[:, h * HALF + k, :], ident[:, :])
                last.then_inc(xT_psum, 1)
            pe.wait_ge(ld_du, 16 * 8)
            T.transpose(bank[6][:, 0:P], down4[:, :], ident[:, :])
            T.transpose(bank[6][:, P:2 * P], up4[:, :, :], ident[:, :])
            pe.wait_ge(ld_vec, 16 * 14)
            T.transpose(bank[6][:, 2 * P:2 * P + NR], vec_rows[:, :],
                        ident[0:NR, 0:NR]).then_inc(small_T, 1)
            pe.wait_ge(small_copied, 1)
            for h in range(2):
                pe.wait_ge(xT_ready, h + 1)
                T.matmul(bank[2 + h][:, :], down4T[:, :], xT[:, h * HC:(h + 1) * HC],
                         start=True, stop=True).then_inc(hid_psum, 1)
            pe.wait_ge(bd_ready, 1)
            for h in range(2):
                for k in range(HALF):
                    t = h * HALF + k
                    last = T.matmul(bank[4 + h][:, k * P:(k + 1) * P],
                                    wg_bd[:, t, :, :], up4T[:, :], start=True, stop=True)
                last.then_inc(g_psum, 1)
            pe.wait_ge(bsumT_ready, 1)
            T.matmul(bank[7][0:B, 0:D], bsumT[:, :], up4T[0:A, :], start=True, stop=True).then_inc(cb_psum, 1)
            pe.wait_ge(cb_ready, 1)
            for h in range(2):
                pe.wait_ge(g_ready, h + 1)
                pe.wait_ge(hid_ready, h + 1)
                for k in range(HALF):
                    t = h * HALF + k
                    o = bank[h][:, k * P:(k + 1) * P]
                    T.matmul(o, batch_of[:, t * P:(t + 1) * P], cb[:, :], start=True, stop=False)
                    last = T.matmul(o, hid_bd[:, t, :], G[:, t, :], start=False, stop=True)
                last.then_inc(o0_psum, 1)
            pe.wait_ge(perm_ready, 1)
            pe.wait_ge(table_ready, 1)
            for t in range(NT):
                last = T.matmul(bank[7][:, P + t * 16:P + t * 16 + NTAB], perm[:, t * P:(t + 1) * P],
                                table[:, :], start=True, stop=True)
            last.then_inc(tab_psum, 1)
            pe.wait_ge(g_ready, 2)
            pe.wait_ge(cond_rep_ready, 1)
            for h in range(2):
                T.matmul(bank[4 + h][:, :], cond_rep[:, :], perm_h[:, h * HC:(h + 1) * HC],
                         start=True, stop=True).then_inc(cond_psum, 1)
            for h in range(2):
                pe.wait_ge(z0_ready, h + 1)
                for k in range(HALF):
                    last = T.transpose(bank[2 + h][:, k * P:(k + 1) * P], z0[:, h * HALF + k, :], ident[:, :])
                last.then_inc(z0T_psum, 1)

            def up(w, par, slot, count):
                pe.wait_ge(ld_wi[slot], 16 * count)
                if not isinstance(w, int) or w >= 2:
                    pe.wait_ge(gelu_done, w - 1)
                s = win_value(pe, 0, w, B * S)
                for c in range(NC1):
                    last = T.matmul(bank[4 + par][:, c * P:(c + 1) * P], wi_st[:, slot, c * P:(c + 1) * P],
                                    x1T[:, bass.ds(s, P)], start=True, stop=True)
                last.then_inc(up_done, 1)

            def down(w, par):
                e = win_value(pe, 1, w, E1 - 1)
                pe.wait_ge(xr_ready, w + 1)
                o = bank[6 + par][:, 0:D]
                T.matmul(o, xrT[:, par, :], ident[:, :], start=True, stop=False)
                pe.wait_ge(gelu_done, w + 1)
                for c in range(NC1):
                    last = T.matmul(o, hT[:, par, c * P:(c + 1) * P],
                                    wo[:, bass.ds(e, 1), c, :],
                                    start=False, stop=(c == NC1 - 1))
                last.then_inc(down_done, 1)

            def backT(w, par):
                pe.wait_ge(z1_ready, w + 1)
                T.transpose(bank[par][:, 0:P], z1[:, par, :], ident[:, :]).then_inc(z1T_done, 1)

            pe.wait_ge(win_ready, 1)
            pe.wait_ge(x1_ready, 1)
            pe.wait_ge(cond_ready, 1)
            pe.wait_ge(tab_ready, 1)
            pe.wait_ge(ld_wo, 32)
            for w in range(NW + 2):
                if w < NW:
                    up(w, w % 2, w % 3, w // 3 + 1)
                if 1 <= w <= NW:
                    down(w - 1, (w - 1) % 2)
                if w >= 2:
                    backT(w - 2, w % 2)

            pe.wait_ge(x2_done, NW)
            pe.wait_ge(ld_l2, 16 * 8)
            BANKS = {("h", 0, 0): 2, ("h", 0, 1): 3, ("h", 0, 2): 4, ("h", 0, 3): 5,
                     ("h", 1, 0): 6, ("h", 1, 1): 7, ("s", 0): 0, ("h", 1, 2): 1, ("h", 1, 3): 2,
                     ("s", 1): 4}

            def first_layer(h, k):
                T.matmul(bank[BANKS["h", h, k]][:, :], w1[:, k, :], x2T[:, h * HC:(h + 1) * HC],
                         start=True, stop=True).then_inc(l2_psum, 1)

            def second_layer(h):
                b = bank[BANKS["s", h]][:, :]
                T.matmul(b, w2s[:, 0, :], h2[:, h, 2, :], start=True, stop=False)
                T.matmul(b, w2s[:, 1, :], h2[:, h, 3, :], start=False, stop=True).then_inc(l2_psum, 1)

            def last_layer(h):
                pe.wait_ge(masked, 3 * h + 3)
                for k in range(HALF):
                    t = h * HALF + k
                    c = slice(k * P, (k + 1) * P)
                    o = bank[3 + 2 * h][:, c]
                    T.matmul(o, x2T[:, t * P:(t + 1) * P], ident[:, :], start=True, stop=False)
                    T.matmul(o, h2[:, h, 0, c], w_last[:, 0, :], start=False, stop=False)
                    T.matmul(o, h2[:, h, 1, c], w_last[:, 1, :], start=False, stop=False)
                    last = T.matmul(o, h3[:, h, c], w_last[:, 2, :], start=False, stop=True)
                last.then_inc(last_psum, 1)

            for k in range(4):
                first_layer(0, k)
            first_layer(1, 0)
            first_layer(1, 1)
            pe.wait_ge(l2_gelu, 4)
            second_layer(0)
            first_layer(1, 2)
            first_layer(1, 3)
            last_layer(0)
            pe.wait_ge(l2_gelu, 9)
            second_layer(1)
            last_layer(1)

        @block.scalar
        def _(act):
            V = nc.scalar
            for r in range(BT):
                act.dma_start(down4[r * A:(r + 1) * A, :], down_W).then_inc(ld_du, 16)
                act.dma_start(up4[:, r, :], up_W).then_inc(ld_du, 16)
            for r0, v in ((R_BI, bi.rearrange("e (c i) -> (e c) i", i=P)), (R_BO, bo), (R_G1, g1), (R_BE1, be1),
                          (R_G0, row(g0)), (R_BE0, row(be0)), (R_NR, row(b1_nr)), (R_TSR, row(b1_tsr)),
                          (R_SR, b1_sr.rearrange("(a b) -> a b", b=P)), (R_SR2, row(b2_sr))):
                act.dma_start(vec_rows[r0:r0 + v.shape[0], :], v).then_inc(ld_vec, 16)
            for r in range(BT):
                act.dma_start(vec_rows[R_DB:R_DB + 1, r * A:(r + 1) * A], row(down_b)).then_inc(ld_vec, 16)
            act.dma_start(up_b_rows[:, :], everywhere(up_b, B)).then_inc(ld_upb, 16)
            act.wait_ge(angles_ready, 1)
            V.activation(table[:, T_COS:T_COS + 8], angles[:, :], ACT.Sin).then_inc(table_ready, 1)
            for h in range(2):
                act.wait_ge(xT_psum, h + 1)
                V.copy(xT[:, h * HC:(h + 1) * HC], bank[h][:, :]).then_inc(xT_ready, 1)
            act.wait_ge(small_copied, 1)
            act.wait_ge(consts, 1)
            for h in range(2):
                act.wait_ge(hid_psum, h + 1)
                for r in range(BT):
                    q = slice(r * A, (r + 1) * A)
                    src = bank[2 + h].rearrange("p (k c) -> p k c", c=P)
                    last = V.activation(hid_bd[q, h * HALF:(h + 1) * HALF, r * S:(r + 1) * S],
                                        src[q, :, r * S:(r + 1) * S], ACT.Gelu, bias=vecT[q, R_DB:R_DB + 1])
                last.then_inc(hid_ready, 1)
            for h in range(2):
                act.wait_ge(g_psum, h + 1)
                V.copy(G[:, h * HALF:(h + 1) * HALF, :], bank[4 + h][:, :]).then_inc(g_ready, 1)
            for k, v in ((0, w1_nr), (1, w1_tsr)):
                act.dma_start(w1[:, k, :], v).then_inc(ld_l2, 16)
            act.dma_start(w1[:, 2:4, :], w1_sr.rearrange("h (c k) -> h c k", k=P)).then_inc(ld_l2, 16)
            act.dma_start(w2s[:, :, :], w2_sr.rearrange("(c h) k -> h c k", h=P)).then_inc(ld_l2, 16)
            for k, v in enumerate((w2_nr, w2_tsr, w3_sr)):
                act.dma_start(w_last[:, k, :], v).then_inc(ld_l2, 16)
            act.dma_start(g2r[:, :], everywhere(g2, P)).then_inc(ld_l2, 16)
            act.dma_start(be2r[:, :], everywhere(be2, P)).then_inc(ld_rows, 16)
            for k, v in enumerate((b2_nr, b2_tsr, b3_sr)):
                act.dma_start(b_last[:, k, :], everywhere(v, P)).then_inc(ld_rows, 16)
            for h in range(2):
                act.wait_ge(cond_psum, h + 1)
                last = V.copy(cond_row[:, h * HC:(h + 1) * HC], bank[4 + h][:, :])
            last.then_inc(cond_ready, 1)
            act.wait_ge(win_ready, 1)
            for w in range(NW):
                e = win_value(act, 1, w, E1 - 1)
                act.wait_ge(up_done, w + 1)
                if w >= 2:
                    act.wait_ge(down_done, w - 1)
                for c in range(NC1):
                    last = V.activation(hT[:, w % 2, c * P:(c + 1) * P], bank[4 + w % 2][:, c * P:(c + 1) * P],
                                        ACT.Gelu, bias=vecT[:, bass.ds(e * NC1 + (R_BI + c), 1)])
                last.then_inc(gelu_done, 1)
            order = [(0, 0, 2, R_NR), (0, 1, 3, R_TSR), (0, 2, 4, R_SR), (0, 3, 5, R_SR + 1),
                     (1, 0, 6, R_NR), (1, 1, 7, R_TSR), (0, 4, 0, R_SR2),
                     (1, 2, 1, R_SR), (1, 3, 2, R_SR + 1), (1, 4, 4, R_SR2)]
            for n, (h, k, b, r) in enumerate(order):
                act.wait_ge(l2_psum, n + 1)
                dst = h3[:, h, :] if k == 4 else h2[:, h, k, :]
                V.activation(dst, bank[b][:, :], ACT.Gelu, bias=vecT[:, r:r + 1]).then_inc(l2_gelu, 1)

        @block.vector
        def _(dve):
            V = nc.vector
            steps = [0]

            def then(ins):
                steps[0] += 1
                ins.then_inc(dstep, 1)
                dve.wait_ge(dstep, steps[0])

            V.memset(x1T[:, B * S:PADDED], 0.0)
            V.memset(rank[:, :], 0.0)
            dve.wait_ge(consts, 1)
            dve.wait_ge(ld_idx, 16 * 5)
            then(V.tensor_scalar(p_int[:, 1:2], p_int[:, 0:1], A - 1, None, ALU.bitwise_and))
            V.tensor_copy(p_mod[:, :], p_int[:, 1:2])
            then(V.tensor_copy(dom_f[:, :], dom_i[:, :]))
            then(V.tensor_tensor(dom_t[:, :, :], dom_f.rearrange("p (t r) -> p t r", r=BT),
                                 quad[:, None, :].to_broadcast([P, NT, BT]), ALU.mult))
            then(V.tensor_reduce(dom_p[:, :], dom_t[:, :, :], AX.X, ALU.add))
            then(V.tensor_scalar(dom_c[:, :], dom_p[:, :], 0.0, float(E0 - 1), ALU.max, ALU.min))
            then(V.tensor_scalar(widx_f[:, :], dom_c[:, :], float(A), p_mod[:, 0:1], ALU.mult, ALU.add))
            V.tensor_copy(widx[:, :], widx_f[:, :]).then_inc(widx_ready, 1)
            V.tensor_copy(domcol[:, 0:1], domcol_i[:, :])
            then(V.tensor_tensor(valid_p[:, :], dom_c[:, :], dom_p[:, :], ALU.is_equal))
            then(V.tensor_scalar(domcol[:, 1:2], domcol[:, 0:1], 0.0, float(E0 - 1), ALU.max, ALU.min))
            V.tensor_copy(domidx[:, :], domcol[:, 1:2]).then_inc(widx_ready, 1)
            V.tensor_tensor(domcol[:, 2:3], domcol[:, 0:1], domcol[:, 1:2], ALU.is_equal)
            V.tensor_copy(exp_f[:, :], exp_i[:, :])
            then(V.tensor_copy(keycol[:, 0:1], expcol_i[:, :]))
            V.scalar_tensor_tensor(keys[:, :], exp_f[0:B, :], float(B), iota_b[:, :], ALU.mult, ALU.add)
            then(V.scalar_tensor_tensor(keycol[:, 1:2], keycol[:, 0:1], float(B), iota_p[:, :], ALU.mult, ALU.add))
            then(V.tensor_scalar(before[:, :], keys[:, :], keycol[:, 1:2], None, ALU.is_lt))
            then(V.tensor_reduce(rank[:, 0:1], before[:, :], AX.X, ALU.add))
            then(V.transpose(rankT[:, :], rank[:, :]))
            V.tensor_scalar(rank_cols[:, :], rankT[0:1, :], float(S), None, ALU.mult).then_inc(ranked, 1)
            V.tensor_scalar(perm[:, :], slot_of[:, :], rank[:, 0:1], None, ALU.is_equal)
            V.tensor_scalar(perm_h[:, :], slot_of[:, :], rank[:, 0:1], None, ALU.is_equal).then_inc(perm_ready, 1)
            V.tensor_copy(table[:, 0:1], iota_p[:, :])
            V.tensor_copy(table[:, T_COND:T_COND + 1], cond_i[:, :])
            dve.wait_ge(ld_ang, 32)
            for i in range(2):
                V.tensor_scalar(angles[:, 2 * i:2 * i + 2], tp[:, i:i + 1].to_broadcast([B, 2]), -1.0, HALF_PI,
                                ALU.mult, ALU.add)
                V.tensor_copy(angles[:, 4 + 2 * i:5 + 2 * i], tp[:, i:i + 1])
                last = V.tensor_scalar(angles[:, 5 + 2 * i:6 + 2 * i], tp[:, i:i + 1], -1.0, None, ALU.mult)
            last.then_inc(angles_ready, 1)
            V.tensor_copy(cond_rep[:, :], cond_i[:, 0:1].to_broadcast([B, P])).then_inc(cond_rep_ready, 1)
            dve.wait_ge(small_T, 1)
            V.tensor_copy(down4T[:, :], bank[6][:, 0:P])
            V.tensor_copy(up4T[:, :], bank[6][:, P:2 * P])
            V.tensor_copy(vecT[:, :], bank[6][:, 2 * P:2 * P + NR]).then_inc(small_copied, 1)

            ex = exp_f[0:1, :]
            then(V.tensor_tensor(c_lt[:, :, :], ex[:, None, :].to_broadcast([1, E1 + 1, B]),
                                 iota_r[:, 0:E1 + 1, None].to_broadcast([1, E1 + 1, B]), ALU.is_lt))
            then(V.tensor_reduce(s_cum[:, :], c_lt[:, :, :], AX.X, ALU.add))
            then(V.tensor_tensor(n_e[:, :], s_cum[:, 1:E1 + 1], s_cum[:, 0:E1], ALU.subtract))
            then(V.scalar_tensor_tensor(c_nw[:, :, :], iota_r[:, None, 0:E1].to_broadcast([1, E1, E1]), float(BT),
                                        n_e[:, :, None].to_broadcast([1, E1, E1]), ALU.mult, ALU.is_lt))
            then(V.tensor_reduce(nw_e[:, :], c_nw[:, :, :], AX.X, ALU.add))
            then(V.tensor_tensor(c_nw[:, :, :], tri[:, :, :], nw_e[:, None, :].to_broadcast([1, E1, E1]), ALU.mult))
            then(V.tensor_reduce(cw[:, :], c_nw[:, :, :], AX.X, ALU.add))
            then(V.tensor_tensor(cwx[:, :], cw[:, :], nw_e[:, :], ALU.subtract))
            then(V.scalar_tensor_tensor(base[:, :], cwx[:, :], -float(BT), s_cum[:, 0:E1], ALU.mult, ALU.add))
            then(V.tensor_tensor(c_w[:, :, :], cw[:, None, :].to_broadcast([1, NW, E1]),
                                 iota_r[:, 0:NW, None].to_broadcast([1, NW, E1]), ALU.is_le))
            then(V.tensor_reduce(e_w[:, :], c_w[:, :, :], AX.X, ALU.add))
            then(V.tensor_tensor(c_w[:, :, :], e_w[:, :, None].to_broadcast([1, NW, E1]),
                                 iota_r[:, None, 0:E1].to_broadcast([1, NW, E1]), ALU.is_equal))
            then(V.tensor_tensor(c_w[:, :, :], c_w[:, :, :], base[:, None, :].to_broadcast([1, NW, E1]), ALU.mult))
            then(V.tensor_reduce(s_w[:, :], c_w[:, :, :], AX.X, ALU.add))
            then(V.scalar_tensor_tensor(s_w[:, :], iota_r[:, 0:NW], float(BT), s_w[:, :], ALU.mult, ALU.add))
            V.tensor_scalar(v_w[:, :], e_w[:, :], float(E1), None, ALU.is_lt)
            then(V.tensor_scalar(s_w[:, :], s_w[:, :], float(S), -float(B * S), ALU.mult, ALU.add))
            then(V.tensor_tensor(s_w[:, :], s_w[:, :], v_w[:, :], ALU.mult))
            V.tensor_scalar(win[:, 0, :], s_w[:, :], float(B * S), None, ALU.add)
            V.tensor_scalar(win[:, 1, :], e_w[:, :], float(E1 - 1), None, ALU.min).then_inc(win_ready, 1)

            V.tensor_scalar(valid_2[:, :], valid_p[:, :], -1.0, 1.0, ALU.mult, ALU.add).then_inc(dstep, 1)
            steps[0] += 1
            dve.wait_ge(dstep, steps[0])
            then(V.tensor_tensor(eye_inv[:, :, :], eye32[:, None, :].to_broadcast([P, NT, A]),
                                 valid_2[:, :, None].to_broadcast([P, NT, A]), ALU.mult))
            dve.wait_ge(ld_wg, 16 * NT)
            then(V.tensor_tensor(wg[:, :, :], wg[:, :, :], valid_p[:, :, None].to_broadcast([P, NT, A]), ALU.mult))
            then(V.tensor_tensor(wg[:, :, :], wg[:, :, :], eye_inv[:, :, :], ALU.add))
            V.tensor_tensor(wg_bd[:, :, :, :], wg[:, :, None, :].to_broadcast([P, NT, BT, A]),
                            quad_o[:, None, :, None].to_broadcast([P, NT, BT, A]), ALU.mult).then_inc(bd_ready, 1)
            dve.wait_ge(ld_eb, 32)
            then(V.scalar_tensor_tensor(bsum[:, :], eb_rows[:, :], domcol[:, 2:3], emb_rows[:, :], ALU.mult, ALU.add))
            V.transpose(bsumT[:, :], bsum[:, :]).then_inc(bsumT_ready, 1)
            dve.wait_ge(ld_upb, 16)
            dve.wait_ge(cb_psum, 1)
            V.tensor_tensor(cb[:, :], bank[7][0:B, 0:D], up_b_rows[:, :], ALU.add).then_inc(cb_ready, 1)

            for h in range(2):
                dve.wait_ge(o0_psum, h + 1)
                ts = slice(h * HALF, (h + 1) * HALF)
                then(V.tensor_tensor(r_sb[:, h, :, :], bank[h].rearrange("p (k c) -> p k c", c=P), x_tok[:, ts, :], ALU.add))
                for k in range(HALF):
                    last = V.bn_stats(stats[:, h, k, :], r_sb[:, h, k, :])
                then(last)
                for k in range(HALF):
                    last = V.bn_aggr(mv[:, h, k, :], stats[:, h, k, :])
                last.then_inc(mv_ready, 1)
                if h == 0:
                    dve.wait_ge(tab_psum, 1)
                    tabs = bank[7][:, P:2 * P].rearrange("p (t n) -> p t n", n=16)
                    then(V.tensor_copy(tok_tab[:, :, :], tabs[:, :, 0:NTAB]))
                    V.tensor_scalar(tok_f[:, :], tok_tab[:, :, 0], float(S), p_mod[:, 0:1], ALU.mult,
                                    ALU.add).then_inc(dstep, 1)
                    steps[0] += 1
                    dve.wait_ge(dstep, steps[0])
                    V.tensor_copy(tok_idx[:, :], tok_f[:, :]).then_inc(tab_ready, 1)
                dve.wait_ge(rstd_ready, h + 1)
                dve.wait_ge(mv_ready, h + 1)
                for k in range(HALF):
                    last = V.tensor_scalar(z0[:, h * HALF + k, :], r_sb[:, h, k, :], mv[:, h, k, 0:1],
                                           rstd[:, h, k:k + 1], ALU.subtract, ALU.mult)
                last.then_inc(z0_ready, 1)
            for h in range(2):
                dve.wait_ge(z0T_psum, h + 1)
                for k in range(HALF * BT):
                    b = h * HALF * BT + k
                    c = dve.value_load(rank_cols[0:1, b:b + 1], min_val=0, max_val=(B - 1) * S)
                    last = V.tensor_scalar(x1T[:, bass.ds(c, S)], bank[2 + h][:, k * S:(k + 1) * S],
                                           vecT[:, R_G0:R_G0 + 1], vecT[:, R_BE0:R_BE0 + 1], ALU.mult, ALU.add)
            last.then_inc(x1_ready, 1)
            dve.wait_ge(x1_ready, 1)

            def residual(w, par):
                s = win_value(dve, 0, w, B * S)
                e = win_value(dve, 1, w, E1 - 1)
                if w >= 2:
                    dve.wait_ge(down_done, w - 1)
                V.tensor_scalar(xrT[:, par, :], x1T[:, bass.ds(s, P)], vecT[:, bass.ds(e + R_BO, 1)], None,
                                ALU.add).then_inc(xr_ready, 1)

            def norm_stats(w, par):
                dve.wait_ge(down_done, w + 1)
                then(V.bn_stats(st1[:, par, :], bank[6 + par][:, 0:D]))
                V.bn_aggr(mv1[:, par, :], st1[:, par, :]).then_inc(mv1_ready, 1)

            def normalize(w, par):
                dve.wait_ge(mv1_ready, w + 1)
                dve.wait_ge(rstd1_ready, w + 1)
                if w >= 2:
                    dve.wait_ge(z1T_done, w - 1)
                V.tensor_scalar(z1[:, par, :], bank[6 + par][:, 0:D], mv1[:, par, 0:1], rstd1[:, par, 0:1],
                                ALU.subtract, ALU.mult).then_inc(z1_ready, 1)

            def scale_shift(w, par):
                s = win_value(dve, 0, w, B * S)
                e = win_value(dve, 1, w, E1 - 1)
                dve.wait_ge(z1T_done, w + 1)
                V.tensor_scalar(x2T[:, bass.ds(s, P)], bank[par][:, 0:P], vecT[:, bass.ds(e + R_G1, 1)],
                                vecT[:, bass.ds(e + R_BE1, 1)], ALU.mult, ALU.add).then_inc(x2_done, 1)
                dve.wait_ge(x2_done, w + 1)

            for w in range(NW + 2):
                if w < NW:
                    residual(w, w % 2)
                if 1 <= w <= NW:
                    norm_stats(w - 1, (w - 1) % 2)
                if w >= 2:
                    scale_shift(w - 2, w % 2)
                if 1 <= w <= NW:
                    normalize(w - 1, (w - 1) % 2)

            def mask(h, c, t, n):
                dve.wait_ge(l2_gelu, n)
                V.scalar_tensor_tensor(t, cond_row[:, h * HC:(h + 1) * HC], float(c), t, ALU.is_equal,
                                       ALU.mult).then_inc(masked, 1)

            def l2_norm(h):
                dve.wait_ge(last_psum, h + 1)
                dve.wait_ge(clast_ready, 1)
                ts = slice(h * HALF, (h + 1) * HALF)
                then(V.tensor_tensor(r_sb[:, h, :, :], bank[3 + 2 * h].rearrange("p (k c) -> p k c", c=P),
                                     c_last[:, ts, :], ALU.add))
                for k in range(HALF):
                    last = V.bn_stats(stats[:, h, k, :], r_sb[:, h, k, :])
                then(last)
                for k in range(HALF):
                    last = V.bn_aggr(mv[:, h, k, :], stats[:, h, k, :])
                last.then_inc(mv_ready, 1)
                dve.wait_ge(rstd_ready, 3 + h)
                dve.wait_ge(mv_ready, 3 + h)
                for k in range(HALF):
                    last = V.tensor_scalar(z2[:, h * HALF + k, :], r_sb[:, h, k, :], mv[:, h, k, 0:1],
                                           rstd[:, h, k:k + 1], ALU.subtract, ALU.mult)
                last.then_inc(z2_ready, 1)
                dve.wait_ge(z2_ready, h + 1)
                dve.wait_ge(rot_ready, 1)
                for k in range(HALF):
                    t = h * HALF + k
                    V.tensor_tensor(y_a[:, t, :], z2[:, t, :], rot_a[:, t, :], ALU.mult).then_inc(dstep, 1)
                    steps[0] += 1
                for k in range(HALF):
                    t = h * HALF + k
                    dve.wait_ge(dstep, steps[0] - HALF + k + 1)
                    dve.wait_ge(yb_ready, t + 1)
                    V.tensor_tensor(y[:, t, :], y_a[:, t, :], y_b[:, t, :], ALU.add).then_inc(y_ready, 1)

            mask(0, 0, h2[:, 0, 0, :], 1)
            mask(0, 1, h2[:, 0, 1, :], 2)
            mask(0, 2, h3[:, 0, :], 7)
            mask(1, 0, h2[:, 1, 0, :], 5)
            mask(1, 1, h2[:, 1, 1, :], 6)
            l2_norm(0)
            mask(1, 2, h3[:, 1, :], 10)
            l2_norm(1)

        @block.gpsimd
        def _(pool):
            V = nc.gpsimd
            steps = [0]

            def then(ins):
                steps[0] += 1
                ins.then_inc(pstep, 1)
                pool.wait_ge(pstep, steps[0])

            V.memset(ident[:, :], 0.0)
            V.memset(quad[:, :], 1.0)
            V.memset(batch_of[:, :], 1.0)
            V.memset(tri[:, :, :], 1.0)
            V.memset(eye32[:, :], 0.0)
            V.memset(mhalf[:, :], -0.5)
            V.iota(iota_b[:, :], [[1, B]], base=0, channel_multiplier=0, allow_small_or_imprecise_dtypes=True)
            V.iota(iota_p[:, :], [[0, 1]], base=0, channel_multiplier=1, allow_small_or_imprecise_dtypes=True)
            V.iota(iota_r[:, :], [[1, B]], base=0, channel_multiplier=0, allow_small_or_imprecise_dtypes=True)
            V.iota(slot_of[:, :], [[1, B], [0, S]], base=0, channel_multiplier=0,
                   allow_small_or_imprecise_dtypes=True)
            V.iota(p_int[:, 0:1], [[0, 1]], base=0, channel_multiplier=1)
            then(V.memset(hid_bd[:, :, :], 0.0))
            V.affine_select(ident[:, :], ident[:, :], [[1, P]], ALU.not_equal, 1.0, base=0, channel_multiplier=-1)
            then(V.affine_select(quad[:, :], quad[:, :], [[-A, BT]], ALU.is_ge, 0.0, base=0, channel_multiplier=1))
            then(V.affine_select(quad[:, :], quad[:, :], [[A, BT]], ALU.is_ge, 0.0, base=A - 1, channel_multiplier=-1))
            V.tensor_copy(quad_o[:, :], quad[:, :])
            then(V.affine_select(batch_of[:, :], batch_of[:, :], [[1, B], [0, S]], ALU.is_equal, 0.0, base=0,
                                 channel_multiplier=-1))
            V.affine_select(tri[:, :, :], tri[:, :, :], [[1, E1], [-1, E1]], ALU.is_ge, 0.0, base=0,
                            channel_multiplier=0)
            for r in range(BT):
                then(V.affine_select(eye32[:, :], eye32[:, :], [[1, A]], ALU.not_equal, 1.0, base=r * A,
                                     channel_multiplier=-1))
            V.memset(vpe[:, :, :], 0.0).then_inc(consts, 1)
            pool.wait_ge(widx_ready, 2)
            ew_rows = expert_W.rearrange("e o a -> (e o) a")
            for t in range(NT):
                pool.indirect_dma_start(out=wg[:, t, :], out_offset=None, in_=ew_rows,
                                        in_offset=bass.IndirectOffsetOnAxis(ap=widx[:, t:t + 1], axis=0)
                                        ).then_inc(ld_wg, 16)
            for dst, src in ((eb_rows, expert_b), (emb_rows, domain_emb)):
                pool.indirect_dma_start(out=dst[:, :], out_offset=None, in_=src,
                                        in_offset=bass.IndirectOffsetOnAxis(ap=domidx[:, 0:1], axis=0)
                                        ).then_inc(ld_eb, 16)

            def rstd_of(n, h, eps):
                pool.wait_ge(mv_ready, n + 1)
                then(V.tensor_scalar(vpe[:, h, :], mv[:, h, :, 1], eps, None, ALU.add))
                V.tensor_tensor(rstd[:, h, :], vpe[:, h, :], mhalf[:, :], ALU.pow).then_inc(rstd_ready, 1)

            for h in range(2):
                rstd_of(h, h, 1e-5)
            for w in range(NW):
                pool.wait_ge(mv1_ready, w + 1)
                then(V.tensor_scalar(vpe1[:, w % 2, :], mv1[:, w % 2, 1:2], 1e-12, None, ALU.add))
                V.tensor_tensor(rstd1[:, w % 2, :], vpe1[:, w % 2, :], mhalf[:, 0:1], ALU.pow).then_inc(rstd1_ready, 1)

            pool.wait_ge(tab_ready, 1)
            pool.wait_ge(ld_rows, 16 * 4)
            pool.wait_ge(ld_l2, 16 * 8)
            pool.wait_ge(cond_ready, 1)
            for k in range(3):
                last = V.tensor_scalar(is_c[:, k, :], tok_tab[:, :, T_COND], float(k), None, ALU.is_equal)
            then(last)
            bc = lambda v: v[:, None, :].to_broadcast([P, NT, D])
            for k, dst in enumerate((c_last, rot_a, rot_b)):
                last = V.tensor_tensor(dst[:, :, :], bc(b_last[:, k, :]),
                                       is_c[:, k, :, None].to_broadcast([P, NT, D]), ALU.mult)
            then(last)
            then(V.tensor_tensor(c_last[:, :, :], c_last[:, :, :], rot_a[:, :, :], ALU.add))
            V.tensor_tensor(c_last[:, :, :], c_last[:, :, :], rot_b[:, :, :], ALU.add).then_inc(clast_ready, 1)
            pool.wait_ge(clast_ready, 1)
            quads = lambda v, t: v.rearrange("p t (q f) -> p t q f", f=4)[:, t, :, :]
            row4 = lambda v: v.rearrange("p (q f) -> p q f", f=4)
            swapped = lambda v: v.rearrange("p (q a f) -> p q a f", a=2, f=2)
            for t in range(NT):
                C = tok_tab[:, t, T_COS:T_COS + 4][:, None, :].to_broadcast([P, D // 4, 4])
                V.tensor_tensor(quads(rot_a, t), row4(g2r), C, ALU.mult)
                V.tensor_tensor(quads(rot_c, t), row4(be2r), C, ALU.mult)
                for f in range(4):
                    g = f ^ 1
                    Sn = tok_tab[:, t, T_SIN + f:T_SIN + f + 1][:, None, :].to_broadcast([P, D // 4, 1])
                    V.tensor_tensor(quads(rot_b, t)[:, :, f:f + 1], row4(g2r)[:, :, g:g + 1], Sn, ALU.mult)
                    last = V.tensor_tensor(quads(rot_t, t)[:, :, f:f + 1], row4(be2r)[:, :, g:g + 1], Sn, ALU.mult)
            then(last)
            V.tensor_tensor(rot_c[:, :, :], rot_c[:, :, :], rot_t[:, :, :], ALU.add).then_inc(rot_ready, 1)
            for h in range(2):
                rstd_of(2 + h, h, 1e-5)
                pool.wait_ge(z2_ready, h + 1)
                pool.wait_ge(rot_ready, 1)
                for k in range(HALF):
                    t = h * HALF + k
                    for f in range(2):
                        pair = lambda v, g: v.rearrange("p t (n f) -> p t n f", f=2)[:, t, :, g:g + 1]
                        last = V.tensor_tensor(pair(y_b, f), pair(z2, 1 - f), pair(rot_b, f), ALU.mult)
                    then(last)
                    V.tensor_tensor(y_b[:, t, :], y_b[:, t, :], rot_c[:, t, :], ALU.add).then_inc(yb_ready, 1)
                for k in range(HALF):
                    t = h * HALF + k
                    pool.wait_ge(y_ready, t + 1)
                    pool.indirect_dma_start(out=out_rows,
                                            out_offset=bass.IndirectOffsetOnAxis(ap=tok_idx[:, t:t + 1], axis=0),
                                            in_=y[:, t, :], in_offset=None).then_inc(stored, 16)


_INS = ['x', 'itok_B_0_15', 'itok_B_0_7', 'itok_B_0_2', 'condB_theta', 'condB_phi',
        'L0_cond_down_W', 'L0_cond_down_b', 'L0_cond_up_W', 'L0_cond_up_b', 'L0_cond_expert_W',
        'L0_cond_expert_b', 'L0_cond_domain_emb', 'L0_cond_ln_gamma', 'L0_cond_ln_beta',
        'L1_cond_Wi', 'L1_cond_bi', 'L1_cond_Wo', 'L1_cond_bo', 'L1_cond_gamma', 'L1_cond_beta',
        'L2_cond_w1_nr', 'L2_cond_b1_nr', 'L2_cond_w2_nr', 'L2_cond_b2_nr',
        'L2_cond_w1_tsr', 'L2_cond_b1_tsr', 'L2_cond_w2_tsr', 'L2_cond_b2_tsr',
        'L2_cond_w1_sr', 'L2_cond_b1_sr', 'L2_cond_w2_sr', 'L2_cond_b2_sr', 'L2_cond_w3_sr', 'L2_cond_b3_sr',
        'L2_cond_gamma', 'L2_cond_beta']


def kernel(**inputs):
    import numpy as np
    import concourse.bacc as bacc
    from concourse.bass_utils import run_bass_kernel_spmd

    nc = bacc.Bacc("TRN2", target_bir_lowering=False, num_devices=1)
    arrays, args = {}, []
    for name in _INS:
        a = np.ascontiguousarray(inputs[name])
        arrays[f"in_{name}"] = a
        args.append(nc.dram_tensor(f"in_{name}", a.shape, mybir.dt.from_np(a.dtype), kind="ExternalInput").ap())
    out = nc.dram_tensor("out_x", (B, S, D), fp32, kind="ExternalOutput").ap()
    conditional_layers(nc, *args, out)
    return run_bass_kernel_spmd(nc, [arrays], core_ids=[0]).results[0]["out_x"]
```

```python
import concourse.bass as bass
from concourse import mybir
from contextlib import ExitStack

fp32 = mybir.dt.float32
i32 = mybir.dt.int32
ACT = mybir.ActivationFunctionType
ALU = mybir.AluOpType
AX = mybir.AxisListType
ENG = mybir.EngineType

P = 128
B, S, D = 32, 32, 128
NT = B * S // P
BT = P // S
HALF = NT // 2
HC = HALF * P
HB = B // 2
A, E0 = 32, 16
E1, I1 = 8, 512
NC1 = I1 // P
NW = (B + (BT - 1) * E1) // BT
PAD = B * S
WARM_UP = 9
NXS = 3
WROW = 8
HALF_PI = 1.5707963267948966
EPS0, EPS1, EPS2 = 1e-5, 1e-12, 1e-5

R_BI, R_BO, R_G1, R_BE1, R_G0, R_BE0, R_NR, R_TSR, R_SR, R_SR2, R_LAST = 0, 32, 40, 48, 56, 57, 58, 59, 60, 62, 63
NR = 66
L2_BANK = {(0, 0): 2, (0, 1): 3, (0, 2): 4, (0, 3): 5, (1, 0): 6, (1, 1): 7, (0, 4): 0,
           (1, 2): 1, (1, 3): 2, (1, 4): 4}
LAST_BANK = (3, 5, 6, 7)
L2_ORDER = [(0, 0), (0, 1), (0, 2), (0, 3), (1, 0), (1, 1), (0, 4), (1, 2), (1, 3), (1, 4)]


def conditional_layers(nc, x, idx_domain, idx_expert, idx_cond, theta, phi,
                       down_W, down_b, up_W, up_b, expert_W, expert_b, domain_emb, g0, be0,
                       Wi, bi, Wo, bo, g1, be1,
                       w1_nr, b1_nr, w2_nr, b2_nr, w1_tsr, b1_tsr, w2_tsr, b2_tsr,
                       w1_sr, b1_sr, w2_sr, b2_sr, w3_sr, b3_sr, g2, be2, out):
    ctx = ExitStack()
    with ctx:
        def sb(name, shape, dt=fp32):
            return ctx.enter_context(nc.sbuf_tensor(name, shape, dt))

        def sem(name):
            return ctx.enter_context(nc.semaphore(name))

        x_tok = sb("x_tok", [P, NT, D])
        xT = sb("xT", [P, NT * P])
        x1T = sb("x1T", [P, PAD + BT * S])
        x2T = sb("x2T", [P, PAD + BT * S])
        x2rT = sb("x2rT", [P, NT * P])
        ident = sb("ident", [P, P])
        vec_rows = sb("vec_rows", [NR, P])
        vecT = sb("vecT", [P, NR])
        down_rows = sb("down_rows", [A, D])
        downT = sb("downT", [P, A])
        down_col = sb("down_col", [A, 1])
        up_rows = sb("up_rows", [P, A])
        upT = sb("upT", [A + 1, D])
        hid = sb("hid", [A, NT * P])
        hid2 = sb("hid2", [A + 1, NT * P])
        dom_i = sb("dom_i", [B, 1], i32)
        dom = sb("dom", [B, 4])
        dom_idx = sb("dom_idx", [B, 1], i32)
        wg = sb("wg", [B, A, A])
        wgT = sb("wgT", [A, A, B])
        eb_rows = sb("eb_rows", [B, A])
        emb_rows = sb("emb_rows", [B, A])
        bsum = sb("bsum", [B, A])
        bsumT = sb("bsumT", [A, B])
        exp_i = sb("exp_i", [B, B], i32)
        exp_f = sb("exp_f", [B, B])
        expcol_i = sb("expcol_i", [B, 1], i32)
        keys = sb("keys", [B, B])
        keycol = sb("keycol", [B, 2])
        before = sb("before", [B, B])
        ones = sb("ones", [B, B])
        iota_r = sb("iota_r", [B, B])
        iota_p = sb("iota_p", [B, 1])
        pad_col = sb("pad_col", [B, BT])
        col_less_pad = sb("col_less_pad", [B, BT, B])
        tri = sb("tri", [B, E1, E1])
        c_lt = sb("c_lt", [B, E1 + 1, B])
        s_cum = sb("s_cum", [B, E1 + 1])
        n_e = sb("n_e", [B, E1])
        c_nw = sb("c_nw", [B, E1, E1])
        nw_e = sb("nw_e", [B, E1])
        c_tri = sb("c_tri", [B, E1, E1])
        cw = sb("cw", [B, E1])
        cwx = sb("cwx", [B, E1])
        base = sb("base", [B, E1])
        c_w = sb("c_w", [B, E1])
        c_s = sb("c_s", [B, E1])
        wv = sb("wv", [B, 6])
        places = sb("places", [B, BT])
        c_slot = sb("c_slot", [B, BT, B])
        slot = sb("slot", [B, BT])
        win_p = sb("win_p", [B, WROW], i32)
        win = sb("win", [1, NW * WROW], i32)
        bat_i = sb("bat_i", [P, B], i32)
        bat = sb("bat", [P, 3, B])
        quad = sb("quad", [P, BT])
        ang_q = sb("ang_q", [P, 2 * NT, BT])
        ang_t = sb("ang_t", [P, 2, NT])
        ang = sb("ang", [P, 8, NT])
        trig = sb("trig", [P, 8, NT])
        last_b = sb("last_b", [P, B])
        c_last = sb("c_last", [P, 2, B])
        mhalf = sb("mhalf", [P, HALF])
        stats = sb("stats", [P, 2, HALF, 6])
        mv = sb("mv", [P, 2, HALF, 2])
        vpe = sb("vpe", [P, 2, HALF])
        rstd = sb("rstd", [P, 2, HALF])
        r_sb = sb("r_sb", [P, NT, D])
        z0 = sb("z0", [P, NT, D])
        wi_st = sb("wi_st", [P, 3, I1])
        wo = sb("wo", [P, E1, NC1, D])
        hT = sb("hT", [P, 2, I1])
        xs = sb("xs", [P, NXS, P])
        xrT = sb("xrT", [P, 2, P])
        z1 = sb("z1", [P, 2, D])
        st1 = sb("st1", [P, 2, 6])
        mv1 = sb("mv1", [P, 2, 2])
        vpe1 = sb("vpe1", [P, 2, 1])
        rstd1 = sb("rstd1", [P, 2, 1])
        w1 = sb("w1", [P, 4, P])
        w2s = sb("w2s", [P, 2, P])
        w_last = sb("w_last", [P, 3, P])
        h2 = sb("h2", [P, 2, 4, HC])
        h3 = sb("h3", [P, 2, HC])
        g2r = sb("g2r", [P, D])
        be2r = sb("be2r", [P, D])
        u2 = sb("u2", [P, NT, D])
        z2 = sb("z2", [P, NT, D])
        y_a = sb("y_a", [P, NT, D])
        y_b = sb("y_b", [P, NT, D])
        y = sb("y", [P, NT, D])

        bank = [ctx.enter_context(nc.psum_tensor(f"bank{i}", [P, 512], fp32)) for i in range(8)]

        ld_dom, ld_exp, ld_bat, ld_cond = sem("ld_dom"), sem("ld_exp"), sem("ld_bat"), sem("ld_cond")
        ld_x = [sem(f"ld_x{i}") for i in range(2)]
        ld_vec, ld_du, ld_dcol, ld_upb = sem("ld_vec"), sem("ld_du"), sem("ld_dcol"), sem("ld_upb")
        ld_wg, ld_eb = sem("ld_wg"), sem("ld_eb")
        ld_wo, ld_l2, ld_rows = sem("ld_wo"), sem("ld_l2"), sem("ld_rows")
        ld_wi = [sem(f"ld_wi{i}") for i in range(3)]
        ld_win = sem("ld_win")
        stored = sem("stored")
        ident_ready, consts = sem("ident_ready"), sem("consts")
        idx_ready, before_ready, rank_psum, win_ready = (
            sem("idx_ready"), sem("before_ready"), sem("rank_psum"), sem("win_ready"))
        angles_ready, trig_ready = sem("angles_ready"), sem("trig_ready")
        small_psum, small_ready = sem("small_psum"), sem("small_ready")
        xT_psum, xT_ready = sem("xT_psum"), sem("xT_ready")
        hid_psum, hid_ready = sem("hid_psum"), sem("hid_ready")
        wgT_ready, hid2_psum, hid2_ready = sem("wgT_ready"), sem("hid2_psum"), sem("hid2_ready")
        o0_psum, mv_ready, rstd_ready = sem("o0_psum"), sem("mv_ready"), sem("rstd_ready")
        z0_ready, z0T_psum, x1_ready = sem("z0_ready"), sem("z0T_psum"), sem("x1_ready")
        xs_ready, up_done, gelu_done, xr_ready, down_done = (
            sem("xs_ready"), sem("up_done"), sem("gelu_done"), sem("xr_ready"), sem("down_done"))
        mv1_ready, rstd1_ready, z1_ready, z1T_done, x2_done = (
            sem("mv1_ready"), sem("rstd1_ready"), sem("z1_ready"), sem("z1T_done"), sem("x2_done"))
        l2_psum, l2_gelu, masked, x2r_ready, last_psum = (
            sem("l2_psum"), sem("l2_gelu"), sem("masked"), sem("x2r_ready"), sem("last_psum"))
        z2_ready, yb_ready, y_ready = sem("z2_ready"), sem("yb_ready"), sem("y_ready")
        u2_ready, ya_ready = sem("u2_ready"), sem("ya_ready")
        dstep = sem("dstep")
        pstep = sem("pstep")

        block = ctx.enter_context(nc.Block())

        def row(v):
            return v.rearrange("(a b) -> a b", a=1)

        def col(v):
            return v.rearrange("(a b) -> a b", b=1)

        def everywhere(v, parts):
            return row(v).to_broadcast([parts, v.shape[0]])

        def tiles(b):
            return bank[b].rearrange("p (k c) -> p k c", c=P)

        def win_values(engine, w, first, n, top):
            return nc.values_load_multi_w_load_instructions(
                win[0:1, w * WROW + first:w * WROW + first + n], engines=[engine], min_val=0, max_val=top,
                skip_runtime_bounds_check_because="computed on chip as sums of one-hot picks, within the range")[1]

        def window_columns(engine, w):
            return win_values(engine, w, 0, BT, PAD + (BT - 1) * S)

        def window_expert(engine, w):
            return win_values(engine, w, BT, 1, E1 - 1)[0]

        def fours(v, t):
            return v.rearrange("p t (q f) -> p t q f", f=4)[:, t, :, :]

        def trig4(k, t):
            return trig[:, None, k:k + 4, t].to_broadcast([P, D // 4, 4])

        def pairs(v, t):
            return v.rearrange("p t (q a f) -> p t q a f", a=2, f=2)[:, t, :, :, :]

        def trig2(f, t):
            return trig[:, None, 4 + f:8:2, t].to_broadcast([P, D // 4, 2])

        x_view = x.rearrange("(t r) s d -> (r s) t d", r=BT)
        out_view = out.rearrange("(t r) s d -> (r s) t d", r=BT)

        @block.sync
        def _(sp):
            sp.dma_start(dom_i[:, :], col(idx_domain)).then_inc(ld_dom, 16)
            sp.dma_start(exp_i[:, :], everywhere(idx_expert, B)).then_inc(ld_exp, 16)
            sp.dma_start(expcol_i[:, :], col(idx_expert)).then_inc(ld_exp, 16)
            for h in range(2):
                sp.dma_start(x_tok[:, h * HALF:(h + 1) * HALF, :],
                             x_view[:, h * HALF:(h + 1) * HALF, :]).then_inc(ld_x[h], 16)
            sp.dma_start(bat_i[:, :], everywhere(idx_cond, P)).then_inc(ld_cond, 16)
            for i, v in enumerate((theta, phi)):
                sp.dma_start(bat[:, 1 + i, :], everywhere(v, P)).then_inc(ld_bat, 16)
            sp.wait_ge(win_ready, 1)
            sp.dma_start(win.rearrange("a (w n) -> a w n", n=WROW), win_p[0:NW, :]).then_inc(ld_win, 16)
            sp.wait_ge(ld_win, 16)

            def load_wi(w):
                e = window_expert(ENG.SP, w)
                if w >= 3:
                    sp.wait_ge(up_done, w - 2)
                sp.dma_start(wi_st[:, w % 3, :],
                             Wi.rearrange("e h i -> (e h) i")[bass.ds(e * P, P), :]).then_inc(ld_wi[w % 3], 16)

            load_wi(0)
            for h in range(2):
                es = slice(h * E1 // 2, (h + 1) * E1 // 2)
                sp.dma_start(wo[:, es, :, :], Wo[es].rearrange("e (c i) h -> i e c h", i=P)).then_inc(ld_wo, 16)
            for w in range(1, NW):
                load_wi(w)
            for h in range(2):
                sp.wait_ge(y_ready, HALF * (h + 1))
                sp.dma_start(out_view[:, h * HALF:(h + 1) * HALF, :],
                             y[:, h * HALF:(h + 1) * HALF, :]).then_inc(stored, 16)
            sp.wait_ge(stored, 32)

        @block.tensor
        def _(pe):
            T = nc.tensor
            pe.wait_ge(ident_ready, 1)
            for _ in range(WARM_UP):
                T.matmul(bank[5][:, 0:P], ident[:, :], ident[:, :], start=True, stop=True)
            pe.wait_ge(before_ready, 1)
            T.matmul(bank[7][0:B, 0:B], ones[:, :], before[:, :], start=True, stop=True).then_inc(rank_psum, 1)
            for h in range(2):
                pe.wait_ge(ld_x[h], 16)
                for k in range(HALF):
                    last = T.transpose(bank[h][:, k * P:(k + 1) * P], x_tok[:, h * HALF + k, :], ident[:, :])
                last.then_inc(xT_psum, 1)
            pe.wait_ge(ld_du, 32)
            T.transpose(bank[6][:, 0:A], down_rows[:, :], ident[0:A, 0:A])
            T.transpose(bank[6][0:A, P:2 * P], up_rows[:, :], ident[:, :]).then_inc(small_psum, 1)
            pe.wait_ge(small_ready, 1)
            for h in range(2):
                pe.wait_ge(xT_ready, h + 1)
                T.matmul(bank[2 + h][0:A, :], downT[:, :], xT[:, h * HC:(h + 1) * HC],
                         start=True, stop=True).then_inc(hid_psum, 1)
            pe.wait_ge(ld_vec, 16 * 13)
            T.transpose(bank[6][:, 2 * P:2 * P + NR], vec_rows[:, :],
                        ident[0:NR, 0:NR]).then_inc(small_psum, 1)
            pe.wait_ge(wgT_ready, 1)
            for h in range(2):
                pe.wait_ge(hid_ready, h + 1)
                for k in range(HB):
                    b = h * HB + k
                    last = T.matmul(bank[4 + h][0:A, k * S:(k + 1) * S], wgT[:, :, b], hid[:, b * S:(b + 1) * S],
                                    start=True, stop=True)
                last.then_inc(hid2_psum, 1)
            for h in range(2):
                pe.wait_ge(hid2_ready, h + 1)
                for k in range(HALF):
                    t = h * HALF + k
                    last = T.matmul(bank[h][:, k * P:(k + 1) * P], hid2[:, t * P:(t + 1) * P], upT[:, :],
                                    start=True, stop=True)
                last.then_inc(o0_psum, 1)
            for h in range(2):
                pe.wait_ge(z0_ready, h + 1)
                for k in range(HALF):
                    last = T.transpose(bank[2 + h][:, k * P:(k + 1) * P], z0[:, h * HALF + k, :], ident[:, :])
                last.then_inc(z0T_psum, 1)

            def up(w):
                pe.wait_ge(ld_wi[w % 3], 16 * (w // 3 + 1))
                pe.wait_ge(xs_ready, w + 1)
                if w >= 2:
                    pe.wait_ge(gelu_done, w - 1)
                for c in range(NC1):
                    last = T.matmul(bank[4 + w % 2][:, c * P:(c + 1) * P], wi_st[:, w % 3, c * P:(c + 1) * P],
                                    xs[:, w % NXS, :], start=True, stop=True)
                last.then_inc(up_done, 1)

            def down(w, e):
                pe.wait_ge(xr_ready, w + 1)
                if w >= 2:
                    pe.wait_ge(z1_ready, w - 1)
                o = bank[6 + w % 2][:, 0:D]
                T.matmul(o, xrT[:, w % 2, :], ident[:, :], start=True, stop=False)
                pe.wait_ge(gelu_done, w + 1)
                for c in range(NC1):
                    last = T.matmul(o, hT[:, w % 2, c * P:(c + 1) * P], wo[:, bass.ds(e, 1), c, :],
                                    start=False, stop=(c == NC1 - 1))
                last.then_inc(down_done, 1)

            def backT(w):
                pe.wait_ge(z1_ready, w + 1)
                if w >= 2:
                    pe.wait_ge(x2_done, w - 1)
                T.transpose(bank[w % 2][:, 0:P], z1[:, w % 2, :], ident[:, :]).then_inc(z1T_done, 1)

            pe.wait_ge(ld_win, 16)
            for w in range(NW + 2):
                if w < NW:
                    e_next = window_expert(ENG.PE, w)
                    up(w)
                if 1 <= w <= NW:
                    if w == 1:
                        pe.wait_ge(ld_wo, 32)
                    down(w - 1, e_now)
                e_now = e_next
                if w >= 2:
                    backT(w - 2)

            pe.wait_ge(x2_done, NW)
            pe.wait_ge(ld_l2, 16 * 7)

            def first_layer(h, k):
                T.matmul(bank[L2_BANK[h, k]][:, :], w1[:, k, :], x2T[:, h * HC:(h + 1) * HC],
                         start=True, stop=True).then_inc(l2_psum, 1)

            def second_layer(h):
                b = bank[L2_BANK[h, 4]][:, :]
                T.matmul(b, w2s[:, 0, :], h2[:, h, 2, :], start=True, stop=False)
                T.matmul(b, w2s[:, 1, :], h2[:, h, 3, :], start=False, stop=True).then_inc(l2_psum, 1)

            def last_layer(h):
                pe.wait_ge(masked, 3 * h + 3)
                pe.wait_ge(x2r_ready, 2)
                for k in range(HALF):
                    t = h * HALF + k
                    c = slice(k * P, (k + 1) * P)
                    o = bank[LAST_BANK[t // 2]][:, (t % 2) * P:(t % 2 + 1) * P]
                    T.matmul(o, x2rT[:, t * P:(t + 1) * P], ident[:, :], start=True, stop=False)
                    T.matmul(o, h2[:, h, 0, c], w_last[:, 0, :], start=False, stop=False)
                    T.matmul(o, h2[:, h, 1, c], w_last[:, 1, :], start=False, stop=False)
                    last = T.matmul(o, h3[:, h, c], w_last[:, 2, :], start=False, stop=True)
                    if t % 2:
                        last.then_inc(last_psum, 1)

            for h, k in L2_ORDER[:6]:
                first_layer(h, k)
            pe.wait_ge(l2_gelu, 4)
            second_layer(0)
            first_layer(1, 2)
            first_layer(1, 3)
            last_layer(0)
            pe.wait_ge(l2_gelu, 9)
            second_layer(1)
            last_layer(1)

        @block.scalar
        def _(act):
            V = nc.scalar
            act.dma_start(down_rows[:, :], down_W).then_inc(ld_du, 16)
            act.dma_start(up_rows[:, :], up_W).then_inc(ld_du, 16)
            act.dma_start(down_col[:, :], col(down_b)).then_inc(ld_dcol, 16)
            act.dma_start(upT[A:A + 1, :], row(up_b)).then_inc(ld_upb, 16)
            for r0, v in ((R_G0, row(g0)), (R_BE0, row(be0)),
                          (R_BI, bi.rearrange("e (c i) -> (e c) i", i=P)), (R_BO, bo), (R_G1, g1), (R_BE1, be1),
                          (R_NR, row(b1_nr)), (R_TSR, row(b1_tsr)),
                          (R_SR, b1_sr.rearrange("(a b) -> a b", b=P)), (R_SR2, row(b2_sr)),
                          (R_LAST, row(b2_nr)), (R_LAST + 1, row(b2_tsr)), (R_LAST + 2, row(b3_sr))):
                act.dma_start(vec_rows[r0:r0 + v.shape[0], :], v).then_inc(ld_vec, 16)
            for h in range(2):
                act.wait_ge(xT_psum, h + 1)
                V.copy(xT[:, h * HC:(h + 1) * HC], bank[h][:, :]).then_inc(xT_ready, 1)
            act.wait_ge(small_psum, 1)
            V.copy(downT[:, :], bank[6][:, 0:A])
            V.copy(upT[0:A, :], bank[6][0:A, P:2 * P]).then_inc(small_ready, 1)
            act.wait_ge(ld_dcol, 16)
            for h in range(2):
                act.wait_ge(hid_psum, h + 1)
                V.activation(hid[:, h * HC:(h + 1) * HC], bank[2 + h][0:A, :], ACT.Gelu,
                             bias=down_col[:, 0:1]).then_inc(hid_ready, 1)
            act.wait_ge(small_psum, 2)
            V.copy(vecT[:, :], bank[6][:, 2 * P:2 * P + NR]).then_inc(small_ready, 1)
            act.wait_ge(angles_ready, 1)
            V.activation(trig[:, :, :], ang[:, :, :], ACT.Sin).then_inc(trig_ready, 1)
            for k, v in ((0, w1_nr), (1, w1_tsr)):
                act.dma_start(w1[:, k, :], v).then_inc(ld_l2, 16)
            act.dma_start(w1[:, 2:4, :], w1_sr.rearrange("h (c k) -> h c k", k=P)).then_inc(ld_l2, 16)
            act.dma_start(w2s[:, :, :], w2_sr.rearrange("(c h) k -> h c k", h=P)).then_inc(ld_l2, 16)
            for k, v in enumerate((w2_nr, w2_tsr, w3_sr)):
                act.dma_start(w_last[:, k, :], v).then_inc(ld_l2, 16)
            for dst, v in ((g2r, g2), (be2r, be2)):
                act.dma_start(dst[:, :], everywhere(v, P)).then_inc(ld_rows, 16)
            act.wait_ge(small_ready, 2)
            act.wait_ge(z0T_psum, 1)
            V.activation(x1T[:, 0:HC], bank[2][:, :], ACT.Identity, bias=vecT[:, R_BE0:R_BE0 + 1],
                         scale=vecT[:, R_G0:R_G0 + 1]).then_inc(x1_ready, 1)
            act.wait_ge(ld_win, 16)
            for w in range(NW + 2):
                if w < NW:
                    e = window_expert(ENG.Activation, w)
                    act.wait_ge(up_done, w + 1)
                    if w >= 2:
                        act.wait_ge(down_done, w - 1)
                    for c in range(NC1):
                        last = V.activation(hT[:, w % 2, c * P:(c + 1) * P],
                                            bank[4 + w % 2][:, c * P:(c + 1) * P],
                                            ACT.Gelu, bias=vecT[:, bass.ds(e * NC1 + (R_BI + c), 1)])
                    last.then_inc(gelu_done, 1)
                if w >= 2 and w % 2:
                    v = w - 2
                    e = window_expert(ENG.Activation, v)
                    cols = window_columns(ENG.Activation, v)
                    act.wait_ge(z1T_done, v + 1)
                    act.wait_ge(x2_done, v)
                    for j, c in enumerate(cols):
                        last = V.activation(x2T[:, bass.ds(c, S)], bank[v % 2][:, j * S:(j + 1) * S], ACT.Identity,
                                            bias=vecT[:, bass.ds(e + R_BE1, 1)], scale=vecT[:, bass.ds(e + R_G1, 1)])
                    last.then_inc(x2_done, 1)
            for n, (h, k) in enumerate(L2_ORDER):
                act.wait_ge(l2_psum, n + 1)
                dst = h3[:, h, :] if k == 4 else h2[:, h, k, :]
                r = (R_NR, R_TSR, R_SR, R_SR + 1, R_SR2)[k]
                V.activation(dst, bank[L2_BANK[h, k]][:, :], ACT.Gelu, bias=vecT[:, r:r + 1]).then_inc(l2_gelu, 1)

        @block.vector
        def _(dve):
            V = nc.vector
            steps = [0]

            def then(ins):
                steps[0] += 1
                ins.then_inc(dstep, 1)
                dve.wait_ge(dstep, steps[0])

            V.memset(x1T[:, PAD:PAD + BT * S], 0.0)
            V.memset(ones[:, :], 1.0)
            V.memset(hid2[A:A + 1, :], 1.0)
            V.memset(win_p[:, :], 0)
            dve.wait_ge(ld_dom, 16)
            then(V.tensor_copy(dom[:, 0:1], dom_i[:, :]))
            then(V.tensor_scalar(dom[:, 1:2], dom[:, 0:1], 0.0, float(E0 - 1), ALU.max, ALU.min))
            V.tensor_copy(dom_idx[:, :], dom[:, 1:2]).then_inc(idx_ready, 1)
            then(V.tensor_tensor(dom[:, 2:3], dom[:, 0:1], dom[:, 1:2], ALU.is_equal))
            V.tensor_scalar(dom[:, 3:4], dom[:, 2:3], -1.0, 1.0, ALU.mult, ALU.add)
            dve.wait_ge(ld_exp, 32)
            dve.wait_ge(consts, 1)
            V.tensor_copy(exp_f[:, :], exp_i[:, :])
            then(V.tensor_copy(keycol[:, 0:1], expcol_i[:, :]))
            V.scalar_tensor_tensor(keys[:, :], exp_f[:, :], float(B), iota_r[:, :], ALU.mult, ALU.add)
            then(V.scalar_tensor_tensor(keycol[:, 1:2], keycol[:, 0:1], float(B), iota_p[:, :], ALU.mult, ALU.add))
            V.tensor_scalar(before[:, :], keys[:, :], keycol[:, 1:2], None, ALU.is_gt).then_inc(before_ready, 1)

            then(V.tensor_tensor(c_lt[:, :, :], exp_f[:, None, :].to_broadcast([B, E1 + 1, B]),
                                 iota_r[:, 0:E1 + 1, None].to_broadcast([B, E1 + 1, B]), ALU.is_lt))
            then(V.tensor_reduce(s_cum[:, :], c_lt[:, :, :], AX.X, ALU.add))
            then(V.tensor_tensor(n_e[:, :], s_cum[:, 1:E1 + 1], s_cum[:, 0:E1], ALU.subtract))
            then(V.scalar_tensor_tensor(c_nw[:, :, :], iota_r[:, None, 0:E1].to_broadcast([B, E1, E1]), float(BT),
                                        n_e[:, :, None].to_broadcast([B, E1, E1]), ALU.mult, ALU.is_lt))
            then(V.tensor_reduce(nw_e[:, :], c_nw[:, :, :], AX.X, ALU.add))
            dve.wait_ge(ld_wg, 16)
            then(V.tensor_scalar(wg[:, :, :], wg[:, :, :], dom[:, 2:3], None, ALU.mult))
            diagonal = wg.rearrange("b o a -> b (o a)")[:, ::A + 1]
            then(V.tensor_scalar(diagonal, diagonal, dom[:, 3:4], None, ALU.add))
            V.transpose(wgT.rearrange("a o b -> a (o b)"), wg.rearrange("b o a -> b (o a)")).then_inc(wgT_ready, 1)
            dve.wait_ge(ld_eb, 32)
            then(V.scalar_tensor_tensor(bsum[:, :], eb_rows[:, :], dom[:, 2:3], emb_rows[:, :], ALU.mult, ALU.add))
            then(V.transpose(bsumT[:, :], bsum[:, :]))
            then(V.tensor_tensor(c_tri[:, :, :], tri[:, :, :], nw_e[:, None, :].to_broadcast([B, E1, E1]), ALU.mult))
            then(V.tensor_reduce(cw[:, :], c_tri[:, :, :], AX.X, ALU.add))
            V.tensor_scalar(c_w[:, :], cw[:, :], iota_p[:, 0:1], None, ALU.is_le)
            then(V.tensor_tensor(cwx[:, :], cw[:, :], nw_e[:, :], ALU.subtract))
            V.scalar_tensor_tensor(base[:, :], cwx[:, :], -float(BT), s_cum[:, 0:E1], ALU.mult, ALU.add)
            then(V.tensor_reduce(wv[:, 0:1], c_w[:, :], AX.X, ALU.add))
            V.tensor_scalar(wv[:, 1:2], wv[:, 0:1], float(E1), None, ALU.is_lt)
            V.tensor_scalar(win_p[:, BT:BT + 1], wv[:, 0:1], float(E1 - 1), None, ALU.min)
            V.tensor_scalar(wv[:, 2:3], iota_p[:, :], float(BT), -float(B), ALU.mult, ALU.add)
            then(V.scalar_tensor_tensor(c_s[:, :], iota_r[:, 0:E1], wv[:, 0:1], base[:, :], ALU.is_equal, ALU.mult))
            then(V.tensor_reduce(wv[:, 3:4], c_s[:, :], AX.X, ALU.add))
            then(V.tensor_tensor(wv[:, 4:5], wv[:, 3:4], wv[:, 2:3], ALU.add))
            then(V.tensor_scalar(wv[:, 5:6], wv[:, 4:5], wv[:, 1:2], float(B), ALU.mult, ALU.add))
            then(V.tensor_scalar(places[:, :], iota_r[:, 0:BT], wv[:, 5:6], None, ALU.add))
            dve.wait_ge(rank_psum, 1)
            then(V.tensor_tensor(c_slot[:, :, :], bank[7][0:B, None, 0:B].to_broadcast([B, BT, B]),
                                 places[:, :, None].to_broadcast([B, BT, B]), ALU.is_equal))
            then(V.tensor_tensor(c_slot[:, :, :], c_slot[:, :, :], col_less_pad[:, :, :], ALU.mult))
            then(V.tensor_reduce(slot[:, :], c_slot[:, :, :], AX.X, ALU.add))
            V.tensor_tensor(win_p[:, 0:BT], slot[:, :], pad_col[:, :], ALU.add).then_inc(win_ready, 1)

            dve.wait_ge(ld_upb, 16)
            for h in range(2):
                dve.wait_ge(hid2_psum, h + 1)
                V.tensor_tensor(hid2[0:A, h * HC:(h + 1) * HC].rearrange("o (b s) -> o b s", s=S),
                                bank[4 + h][0:A, :].rearrange("o (b s) -> o b s", s=S),
                                bsumT[:, h * HB:(h + 1) * HB, None].to_broadcast([A, HB, S]),
                                ALU.add).then_inc(hid2_ready, 1)

            dve.wait_ge(ld_bat, 32)
            then(V.tensor_tensor(ang_q[:, :, :], bat[:, 1:3, :].rearrange("p n (t r) -> p (n t) r", r=BT),
                                 quad[:, None, :].to_broadcast([P, 2 * NT, BT]), ALU.mult))
            then(V.tensor_reduce(ang_t.rearrange("p n t -> p (n t)"), ang_q[:, :, :], AX.X, ALU.add))
            for i in range(2):
                V.tensor_scalar(ang[:, 2 * i:2 * i + 2, :], ang_t[:, i:i + 1, :].to_broadcast([P, 2, NT]),
                                -1.0, HALF_PI, ALU.mult, ALU.add)
                V.tensor_copy(ang[:, 4 + 2 * i, :], ang_t[:, i, :])
                last = V.tensor_scalar(ang[:, 5 + 2 * i, :], ang_t[:, i, :], -1.0, None, ALU.mult)
            last.then_inc(angles_ready, 1)

            def statistics(n, h, b, residual):
                t0 = h * HALF
                if residual is not None:
                    then(V.tensor_tensor(r_sb[:, t0:t0 + HALF, :], tiles(b), residual, ALU.add))
                for k in range(HALF):
                    src = tiles(b)[:, k, :] if residual is None else r_sb[:, t0 + k, :]
                    last = V.bn_stats(stats[:, h, k, :], src)
                then(last)
                for k in range(HALF):
                    last = V.bn_aggr(mv[:, h, k, :], stats[:, h, k, :])
                last.then_inc(mv_ready, 1)

            for h in range(2):
                dve.wait_ge(o0_psum, h + 1)
                statistics(h, h, h, x_tok[:, h * HALF:(h + 1) * HALF, :])
            for h in range(2):
                dve.wait_ge(rstd_ready, h + 1)
                dve.wait_ge(mv_ready, h + 1)
                for k in range(HALF):
                    t = h * HALF + k
                    last = V.tensor_scalar(z0[:, t, :], r_sb[:, t, :], mv[:, h, k, 0:1], rstd[:, h, k:k + 1],
                                           ALU.subtract, ALU.mult)
                last.then_inc(z0_ready, 1)
            dve.wait_ge(small_ready, 2)
            dve.wait_ge(z0T_psum, 2)
            V.tensor_scalar(x1T[:, HC:2 * HC], bank[3][:, :], vecT[:, R_G0:R_G0 + 1],
                            vecT[:, R_BE0:R_BE0 + 1], ALU.mult, ALU.add).then_inc(x1_ready, 1)

            dve.wait_ge(ld_cond, 16)
            then(V.tensor_copy(bat[:, 0, :], bat_i[:, :]))
            then(V.tensor_scalar(last_b[:, :], bat[:, 0, :], 0.0, vecT[:, R_LAST:R_LAST + 1], ALU.is_equal, ALU.mult))
            for c in (1, 2):
                then(V.tensor_scalar(c_last[:, c - 1, :], bat[:, 0, :], float(c),
                                     vecT[:, R_LAST + c:R_LAST + c + 1], ALU.is_equal, ALU.mult))
                then(V.tensor_tensor(last_b[:, :], last_b[:, :], c_last[:, c - 1, :], ALU.add))
            def residual(w, e):
                dve.wait_ge(xs_ready, w + 1)
                if w >= 2:
                    dve.wait_ge(down_done, w - 1)
                V.tensor_scalar(xrT[:, w % 2, :], xs[:, w % NXS, :], vecT[:, bass.ds(e + R_BO, 1)], None,
                                ALU.add).then_inc(xr_ready, 1)

            def norm_stats(w):
                dve.wait_ge(down_done, w + 1)
                then(V.bn_stats(st1[:, w % 2, :], bank[6 + w % 2][:, 0:D]))
                V.bn_aggr(mv1[:, w % 2, :], st1[:, w % 2, :]).then_inc(mv1_ready, 1)

            def normalize(w):
                dve.wait_ge(mv1_ready, w + 1)
                dve.wait_ge(rstd1_ready, w + 1)
                if w >= 2:
                    dve.wait_ge(z1T_done, w - 1)
                V.tensor_scalar(z1[:, w % 2, :], bank[6 + w % 2][:, 0:D], mv1[:, w % 2, 0:1],
                                rstd1[:, w % 2, 0:1], ALU.subtract, ALU.mult).then_inc(z1_ready, 1)

            def scatter(w, e, cols):
                dve.wait_ge(z1T_done, w + 1)
                if w:
                    dve.wait_ge(x2_done, w)
                for j, c in enumerate(cols):
                    last = V.tensor_scalar(x2T[:, bass.ds(c, S)], bank[w % 2][:, j * S:(j + 1) * S],
                                           vecT[:, bass.ds(e + R_G1, 1)], vecT[:, bass.ds(e + R_BE1, 1)],
                                           ALU.mult, ALU.add)
                last.then_inc(x2_done, 1)

            dve.wait_ge(ld_win, 16)
            for w in range(NW + 2):
                if w < NW:
                    residual(w, window_expert(ENG.DVE, w))
                if 1 <= w <= NW:
                    norm_stats(w - 1)
                if w >= 2 and w % 2 == 0:
                    scatter(w - 2, window_expert(ENG.DVE, w - 2), window_columns(ENG.DVE, w - 2))
                if 1 <= w <= NW:
                    normalize(w - 1)

            def mask(h, c, t, n):
                dve.wait_ge(l2_gelu, n)
                t3 = t.rearrange("p (b s) -> p b s", s=S)
                V.scalar_tensor_tensor(t3, bat[:, 0, h * HB:(h + 1) * HB, None].to_broadcast([P, HB, S]), float(c),
                                       t3, ALU.is_equal, ALU.mult).then_inc(masked, 1)

            def l2_stats(g):
                dve.wait_ge(last_psum, g + 1)
                h, k0 = g // 2, 2 * (g % 2)
                for k in range(2):
                    last = V.bn_stats(stats[:, h, k0 + k, :], tiles(LAST_BANK[g])[:, k, :])
                then(last)
                for k in range(2):
                    last = V.bn_aggr(mv[:, h, k0 + k, :], stats[:, h, k0 + k, :])
                last.then_inc(mv_ready, 1)
                dve.wait_ge(mv_ready, 3 + g)
                dve.wait_ge(ld_rows, 32)
                for k in range(2):
                    V.scalar_tensor_tensor(u2[:, 2 * g + k, :], tiles(LAST_BANK[g])[:, k, :],
                                           mv[:, h, k0 + k, 0:1], g2r[:, :], ALU.subtract, ALU.mult
                                           ).then_inc(u2_ready, 1)

            def l2_out(g):
                h, k0 = g // 2, 2 * (g % 2)
                dve.wait_ge(rstd_ready, 3 + g)
                for k in range(2):
                    t = 2 * g + k
                    dve.wait_ge(u2_ready, t + 1)
                    V.scalar_tensor_tensor(z2[:, t, :], u2[:, t, :], rstd[:, h, k0 + k:k0 + k + 1], be2r[:, :],
                                           ALU.mult, ALU.add).then_inc(z2_ready, 1)
                dve.wait_ge(trig_ready, 1)
                for k in range(2):
                    t = 2 * g + k
                    dve.wait_ge(z2_ready, t + 1)
                    V.tensor_tensor(fours(y_a, t), fours(z2, t), trig4(0, t), ALU.mult).then_inc(ya_ready, 1)
                for k in range(2):
                    t = 2 * g + k
                    dve.wait_ge(ya_ready, t + 1)
                    dve.wait_ge(yb_ready, t + 1)
                    V.tensor_tensor(y[:, t, :], y_a[:, t, :], y_b[:, t, :], ALU.add).then_inc(y_ready, 1)

            for h in range(2):
                dve.wait_ge(x2_done, NW)
                V.tensor_tensor(x2rT[:, h * HC:(h + 1) * HC].rearrange("p (b s) -> p b s", s=S),
                                x2T[:, h * HC:(h + 1) * HC].rearrange("p (b s) -> p b s", s=S),
                                last_b[:, h * HB:(h + 1) * HB, None].to_broadcast([P, HB, S]),
                                ALU.add).then_inc(x2r_ready, 1)
            mask(0, 0, h2[:, 0, 0, :], 1)
            mask(0, 1, h2[:, 0, 1, :], 2)
            mask(0, 2, h3[:, 0, :], 7)
            mask(1, 0, h2[:, 1, 0, :], 5)
            mask(1, 1, h2[:, 1, 1, :], 6)
            l2_stats(0)
            l2_stats(1)
            mask(1, 2, h3[:, 1, :], 10)
            l2_out(0)
            l2_out(1)
            l2_stats(2)
            l2_stats(3)
            l2_out(2)
            l2_out(3)

        @block.gpsimd
        def _(pool):
            V = nc.gpsimd
            steps = [0]

            def then(ins):
                steps[0] += 1
                ins.then_inc(pstep, 1)
                pool.wait_ge(pstep, steps[0])

            V.memset(quad[:, :], 1.0)
            V.memset(mhalf[:, :], -0.5)
            V.memset(tri[:, :, :], 1.0)
            then(V.memset(ident[:, :], 0.0))
            V.affine_select(ident[:, :], ident[:, :], [[1, P]], ALU.not_equal, 1.0, base=0,
                            channel_multiplier=-1).then_inc(ident_ready, 1)
            V.iota(iota_r[:, :], [[1, B]], base=0, channel_multiplier=0, allow_small_or_imprecise_dtypes=True)
            V.iota(iota_p[:, :], [[0, 1]], base=0, channel_multiplier=1, allow_small_or_imprecise_dtypes=True)
            V.iota(pad_col[:, :], [[S, BT]], base=PAD, channel_multiplier=0, allow_small_or_imprecise_dtypes=True)
            V.iota(col_less_pad[:, :, :], [[-S, BT], [S, B]], base=-PAD, channel_multiplier=0,
                   allow_small_or_imprecise_dtypes=True)
            V.affine_select(tri[:, :, :], tri[:, :, :], [[1, E1], [-1, E1]], ALU.is_ge, 0.0, base=0,
                            channel_multiplier=0)
            then(V.affine_select(quad[:, :], quad[:, :], [[-S, BT]], ALU.is_ge, 0.0, base=0, channel_multiplier=1))
            V.affine_select(quad[:, :], quad[:, :], [[S, BT]], ALU.is_ge, 0.0, base=S - 1,
                            channel_multiplier=-1).then_inc(consts, 1)
            pool.wait_ge(idx_ready, 1)
            for dst, src, done in ((wg.rearrange("b o a -> b (o a)"), expert_W.rearrange("e o a -> e (o a)"), ld_wg),
                                   (eb_rows, expert_b, ld_eb), (emb_rows, domain_emb, ld_eb)):
                pool.indirect_dma_start(out=dst[:, :], out_offset=None, in_=src,
                                        in_offset=bass.IndirectOffsetOnAxis(ap=dom_idx[:, 0:1], axis=0)
                                        ).then_inc(done, 16)

            def rstd_of(n, h, ks, eps):
                pool.wait_ge(mv_ready, n + 1)
                then(V.tensor_scalar(vpe[:, h, ks], mv[:, h, ks, 1], eps, None, ALU.add))
                V.tensor_tensor(rstd[:, h, ks], vpe[:, h, ks], mhalf[:, ks], ALU.pow).then_inc(rstd_ready, 1)

            for h in range(2):
                rstd_of(h, h, slice(0, HALF), EPS0)

            pool.wait_ge(ld_win, 16)
            pool.wait_ge(x1_ready, 2)

            def gather(w):
                cols = window_columns(ENG.Pool, w)
                if w >= NXS:
                    pool.wait_ge(up_done, w - NXS + 1)
                    pool.wait_ge(xr_ready, w - NXS + 1)
                for j, c in enumerate(cols):
                    last = V.tensor_copy(xs[:, w % NXS, j * S:(j + 1) * S], x1T[:, bass.ds(c, S)])
                last.then_inc(xs_ready, 1)

            for w in range(NXS - 1):
                gather(w)
            for w in range(NW):
                if w + NXS - 1 < NW and w == 0:
                    gather(NXS - 1)
                pool.wait_ge(mv1_ready, w + 1)
                then(V.tensor_scalar(vpe1[:, w % 2, :], mv1[:, w % 2, 1:2], EPS1, None, ALU.add))
                V.tensor_tensor(rstd1[:, w % 2, :], vpe1[:, w % 2, :], mhalf[:, 0:1], ALU.pow).then_inc(rstd1_ready, 1)
                if w + NXS < NW:
                    gather(w + NXS)
            pool.wait_ge(trig_ready, 1)
            for g in range(NT // 2):
                rstd_of(2 + g, g // 2, slice(2 * (g % 2), 2 * (g % 2) + 2), EPS2)
                for t in (2 * g, 2 * g + 1):
                    pool.wait_ge(z2_ready, t + 1)
                    for f in range(2):
                        last = V.tensor_tensor(pairs(y_b, t)[:, :, :, f], pairs(z2, t)[:, :, :, 1 - f],
                                               trig2(f, t), ALU.mult)
                    last.then_inc(yb_ready, 1)


_INS = ['x', 'itok_B_0_15', 'itok_B_0_7', 'itok_B_0_2', 'condB_theta', 'condB_phi',
        'L0_cond_down_W', 'L0_cond_down_b', 'L0_cond_up_W', 'L0_cond_up_b', 'L0_cond_expert_W',
        'L0_cond_expert_b', 'L0_cond_domain_emb', 'L0_cond_ln_gamma', 'L0_cond_ln_beta',
        'L1_cond_Wi', 'L1_cond_bi', 'L1_cond_Wo', 'L1_cond_bo', 'L1_cond_gamma', 'L1_cond_beta',
        'L2_cond_w1_nr', 'L2_cond_b1_nr', 'L2_cond_w2_nr', 'L2_cond_b2_nr',
        'L2_cond_w1_tsr', 'L2_cond_b1_tsr', 'L2_cond_w2_tsr', 'L2_cond_b2_tsr',
        'L2_cond_w1_sr', 'L2_cond_b1_sr', 'L2_cond_w2_sr', 'L2_cond_b2_sr', 'L2_cond_w3_sr', 'L2_cond_b3_sr',
        'L2_cond_gamma', 'L2_cond_beta']


def kernel(**inputs):
    import numpy as np
    import concourse.bacc as bacc
    from concourse.bass_utils import run_bass_kernel_spmd

    nc = bacc.Bacc("TRN2", target_bir_lowering=False, num_devices=1)
    arrays, args = {}, []
    for name in _INS:
        a = np.ascontiguousarray(inputs[name])
        arrays[f"in_{name}"] = a
        args.append(nc.dram_tensor(f"in_{name}", a.shape, mybir.dt.from_np(a.dtype), kind="ExternalInput").ap())
    out = nc.dram_tensor("out_x", (B, S, D), fp32, kind="ExternalOutput").ap()
    conditional_layers(nc, *args, out)
    return run_bass_kernel_spmd(nc, [arrays], core_ids=[0]).results[0]["out_x"]
```

```python
import concourse.bass as bass
from concourse import mybir
from contextlib import ExitStack

fp32 = mybir.dt.float32
i32 = mybir.dt.int32
ACT = mybir.ActivationFunctionType
ALU = mybir.AluOpType
AX = mybir.AxisListType
ENG = mybir.EngineType

P = 128
B, S, D = 32, 32, 128
NT = B * S // P
BT = P // S
HALF = NT // 2
HC = HALF * P
HB = B // 2
A, E0 = 32, 16
E1, I1 = 8, 512
NC1 = I1 // P
NW = (B + (BT - 1) * E1) // BT
PAD = B * S
WARM_UP = 6
GELU_WAIT = 4
BIAS_WAIT = 1
L0_WAITS = (2, 2, 2, 6)
L1_WAITS = (7, 0, 3)
LAG = 3
NXS = 4
WROW = 8
HALF_PI = 1.5707963267948966
TWO_PI_HIGH = 6.28125
TWO_PI_LOW = 4 * HALF_PI - TWO_PI_HIGH
ROUND = 1.5 * 2.0 ** 23
EPS0, EPS1, EPS2 = 1e-5, 1e-12, 1e-5

R_BI, R_BO, R_G1, R_BE1, R_G0, R_BE0, R_NR, R_TSR, R_SR, R_SR2, R_LAST = 0, 32, 40, 48, 56, 57, 58, 59, 60, 62, 63
NR = 66
L2_BANK = {(0, 0): 2, (0, 1): 3, (0, 2): 4, (0, 3): 5, (1, 0): 6, (1, 1): 7, (0, 4): 0,
           (1, 2): 1, (1, 3): 2, (1, 4): 4}
GROUPS_0 = ((0, 1), (2, 3), (4, 5), (6, 7))
GROUPS_2 = ((0, 1), (2, 3), (4, 5), (6,), (7,))
LAST_BANK = (3, 5, 6, 7, 0)
POOL_SINES = 0
POOL_SUM = 2
L0_BANK = (0, 2, 1, 3)
Z0T_BANK = (4, 5, 6, 7)
L2_ORDER = [(0, 0), (0, 1), (0, 2), (0, 3), (1, 0), (1, 1), (0, 4), (1, 2), (1, 3), (1, 4)]


def conditional_layers(nc, x, idx_domain, idx_expert, idx_cond, theta, phi,
                       down_W, down_b, up_W, up_b, expert_W, expert_b, domain_emb, g0, be0,
                       Wi, bi, Wo, bo, g1, be1,
                       w1_nr, b1_nr, w2_nr, b2_nr, w1_tsr, b1_tsr, w2_tsr, b2_tsr,
                       w1_sr, b1_sr, w2_sr, b2_sr, w3_sr, b3_sr, g2, be2, out):
    ctx = ExitStack()
    with ctx:
        def sb(name, shape, dt=fp32):
            return ctx.enter_context(nc.sbuf_tensor(name, shape, dt))

        def sem(name):
            return ctx.enter_context(nc.semaphore(name))

        x_tok = sb("x_tok", [P, NT, D])
        xT = sb("xT", [P, NT * P])
        x1T = sb("x1T", [P, PAD + NW * BT * S])
        x2T = sb("x2T", [P, PAD + NW * BT * S])
        x2rT = sb("x2rT", [P, NT * P])
        ident = sb("ident", [P, P])
        center = sb("center", [P, P])
        vec_rows = sb("vec_rows", [NR, P])
        vecT = sb("vecT", [P, NR])
        down_rows = sb("down_rows", [A, D])
        downT = sb("downT", [P, A])
        down_col = sb("down_col", [A, 1])
        up_rows = sb("up_rows", [P, A])
        upT = sb("upT", [A + 1, D])
        upT_c = sb("upT_c", [A + 1, D])
        up_sum = sb("up_sum", [A + 1, 1])
        up_mean = sb("up_mean", [A + 1, 1])
        hid = sb("hid", [A, NT * P])
        hid2 = sb("hid2", [A + 1, NT * P])
        dom_i = sb("dom_i", [B, 1], i32)
        dom = sb("dom", [B, 4])
        dom_idx = sb("dom_idx", [B, 1], i32)
        wg = sb("wg", [B, A, A])
        wgT = sb("wgT", [A, A, B])
        eb_rows = sb("eb_rows", [B, A])
        emb_rows = sb("emb_rows", [B, A])
        bsum = sb("bsum", [B, A])
        bsumT = sb("bsumT", [A, B])
        exp_i = sb("exp_i", [B, B], i32)
        exp_f = sb("exp_f", [B, B])
        expcol_i = sb("expcol_i", [B, 1], i32)
        keys = sb("keys", [B, B])
        keycol = sb("keycol", [B, 2])
        before = sb("before", [B, B + E1 + 1])
        ones = sb("ones", [B, B])
        iota_r = sb("iota_r", [B, B])
        iota_p = sb("iota_p", [B, 1])
        place_32 = sb("place_32", [B, BT])
        win_place = sb("win_place", [B, 1])
        pad_col = sb("pad_col", [B, BT])
        col_less_pad = sb("col_less_pad", [B, BT, B])
        tri = sb("tri", [B, E1, E1])
        first = sb("first", [B, E1 + 1])
        n_e = sb("n_e", [B, E1])
        c_nw = sb("c_nw", [B, E1, E1])
        nw_e = sb("nw_e", [B, E1])
        c_tri = sb("c_tri", [B, E1, E1])
        cw = sb("cw", [B, E1])
        cwx = sb("cwx", [B, E1])
        n_left = sb("n_left", [B, E1])
        by_e = sb("by_e", [B, 2, E1])
        taken = sb("taken", [B, BT])
        c_w = sb("c_w", [B, E1])
        c_s = sb("c_s", [B, 2, E1])
        wv = sb("wv", [B, 3])
        places = sb("places", [B, BT])
        c_slot = sb("c_slot", [B, BT, B])
        slot = sb("slot", [B, BT])
        win_p = sb("win_p", [B, WROW], i32)
        win = sb("win", [1, NW * WROW], i32)
        bat_i = sb("bat_i", [P, B], i32)
        bat = sb("bat", [P, 2, B])
        quad = sb("quad", [P, BT])
        ang_q = sb("ang_q", [P, 2 * NT, BT])
        ang = sb("ang", [P, 4, NT])
        turns = sb("turns", [P, 4, NT])
        whole = sb("whole", [P, 4, NT])
        trig = sb("trig", [P, 8, NT])
        cond = sb("cond", [P, B])
        holds = sb("holds", [P, 3, B])
        last_b = sb("last_b", [P, B])
        warm = sb("warm", [1, 4])
        mhalf = sb("mhalf", [P, 3])
        squares = sb("squares", [P, NT, D])
        sumsq = sb("sumsq", [P, NT])
        vpe = sb("vpe", [P, NT])
        rstd = sb("rstd", [P, NT])
        z0 = sb("z0", [P, NT, D])
        wi_st = sb("wi_st", [P, 3, I1])
        wo = sb("wo", [P, E1, NC1, D])
        hT = sb("hT", [P, 2, I1])
        xs = sb("xs", [P, NXS, P])
        xrT = sb("xrT", [P, 2, P])
        z1 = sb("z1", [P, LAG, D])
        st1 = sb("st1", [P, 2, 6])
        mv1 = sb("mv1", [P, 2, 2])
        vpe1 = sb("vpe1", [P, 2, 1])
        rstd1 = sb("rstd1", [P, 2, 1])
        w1 = sb("w1", [P, 4, P])
        w2s = sb("w2s", [P, 2, P])
        w_last = sb("w_last", [P, 3, P])
        w_sum = sb("w_sum", [P, 3])
        w_mean = sb("w_mean", [P, 3])
        w_last_c = sb("w_last_c", [P, 3, P])
        h2 = sb("h2", [P, 2, 4, HC])
        h3 = sb("h3", [P, 2, HC])
        g2r = sb("g2r", [P, D])
        be2r = sb("be2r", [P, D])
        u2 = sb("u2", [P, NT, D])
        z2 = sb("z2", [P, NT, D])
        y_a = sb("y_a", [P, NT, D])
        y_b = sb("y_b", [P, NT, D])
        y = sb("y", [P, NT, D])

        bank = [ctx.enter_context(nc.psum_tensor(f"bank{i}", [P, 512], fp32)) for i in range(8)]

        ld_dom, ld_exp, ld_bat, ld_cond = sem("ld_dom"), sem("ld_exp"), sem("ld_bat"), sem("ld_cond")
        ld_x = [sem(f"ld_x{i}") for i in range(2)]
        ld_vec, ld_du, ld_dcol, ld_upb = sem("ld_vec"), sem("ld_du"), sem("ld_dcol"), sem("ld_upb")
        ld_wg, ld_eb = sem("ld_wg"), sem("ld_eb")
        ld_wo, ld_l2, ld_rows = sem("ld_wo"), sem("ld_l2"), sem("ld_rows")
        ld_wi = [sem(f"ld_wi{i}") for i in range(3)]
        ld_win = sem("ld_win")
        stored = sem("stored")
        ident_ready, warm_ready, consts, late_consts = (
            sem("ident_ready"), sem("warm_ready"), sem("consts"), sem("late_consts"))
        idx_ready, before_ready, rank_psum, win_ready = (
            sem("idx_ready"), sem("before_ready"), sem("rank_psum"), sem("win_ready"))
        angles_ready, trig_ready, last_b_ready = sem("angles_ready"), sem("trig_ready"), sem("last_b_ready")
        small_psum, small_ready = sem("small_psum"), sem("small_ready")
        xT_psum, xT_ready = sem("xT_psum"), sem("xT_ready")
        hid_psum, hid_ready = sem("hid_psum"), sem("hid_ready")
        wgT_ready, hid2_psum, hid2_ready = sem("wgT_ready"), sem("hid2_psum"), sem("hid2_ready")
        center_ready = sem("center_ready")
        up_sum_ready, up_ready, w_last_ready = sem("up_sum_ready"), sem("up_ready"), sem("w_last_ready")
        o0_psum, sumsq_ready, rstd_ready = sem("o0_psum"), sem("sumsq_ready"), sem("rstd_ready")
        z0_ready, z0T_psum, x1_ready = sem("z0_ready"), sem("z0T_psum"), sem("x1_ready")
        xs0_ready = sem("xs0_ready")
        xs_ready, up_done, gelu_done, xr_ready, down_done = (
            sem("xs_ready"), sem("up_done"), sem("gelu_done"), sem("xr_ready"), sem("down_done"))
        mv1_ready, rstd1_ready, z1_ready, z1T_done, x2_dve, x2_act = (
            sem("mv1_ready"), sem("rstd1_ready"), sem("z1_ready"), sem("z1T_done"), sem("x2_dve"), sem("x2_act"))
        l2_psum, l2_gelu, masked_01, masked_2, x2r_ready, last_psum = (
            sem("l2_psum"), sem("l2_gelu"), sem("masked_01"), sem("masked_2"), sem("x2r_ready"), sem("last_psum"))
        z2_ready, yb_ready, yb_dve_ready, y_ready, y_pool_ready = (
            sem("z2_ready"), sem("yb_ready"), sem("yb_dve_ready"), sem("y_ready"), sem("y_pool_ready"))
        ya_ready = sem("ya_ready")
        dstep = sem("dstep")
        pstep = sem("pstep")

        block = ctx.enter_context(nc.Block())

        def row(v):
            return v.rearrange("(a b) -> a b", a=1)

        def col(v):
            return v.rearrange("(a b) -> a b", b=1)

        def everywhere(v, parts):
            return row(v).to_broadcast([parts, v.shape[0]])

        def tiles(b):
            return bank[b].rearrange("p (k c) -> p k c", c=P)

        def group_tile(groups, banks, t):
            g = [t in group for group in groups].index(True)
            return tiles(banks[g])[:, groups[g].index(t), :]

        def tile0(t):
            return group_tile(GROUPS_0, L0_BANK, t)

        def z0T(t):
            return group_tile(GROUPS_0, Z0T_BANK, t)

        def tile2(t):
            return group_tile(GROUPS_2, LAST_BANK, t)

        def up_chunk(w, c):
            return bank[2 + 2 * (w % 2) + c // 2][:, (c % 2) * P:(c % 2 + 1) * P]

        def win_values(engine, w, first, n, top):
            return nc.values_load_multi_w_load_instructions(
                win[0:1, bass.ds(w * WROW + first, n)], engines=[engine], min_val=0, max_val=top,
                skip_runtime_bounds_check_because="computed on chip as sums of one-hot picks, within the range")[1]

        def window_columns(engine, w, slots=range(BT)):
            return win_values(engine, w, slots[0], len(slots), PAD + (NW * BT - 1) * S)

        def slots(w, n):
            if w >= NW - 2:
                return range(n * BT // 2, (n + 1) * BT // 2)
            return range(BT if w % 2 == n else 0)

        def z1T(w, n, slots):
            b = w % 2 if w < NW - 2 else 4 * n + w % 2
            return bank[b][:, slots[0] * S:(slots[-1] + 1) * S]

        def scattered(w, n):
            return sum(len(slots(v, n)) > 0 for v in range(w + 1))

        def window_expert(engine, w):
            return win_values(engine, w, BT, 1, E1 - 1)[0]

        def fours(v, t):
            return v.rearrange("p t (q f) -> p t q f", f=4)[:, t, :, :]

        def trig4(k, t):
            return trig[:, None, k:k + 4, t].to_broadcast([P, D // 4, 4])

        def pairs(v, t):
            return v.rearrange("p t (q a f) -> p t q a f", a=2, f=2)[:, t, :, :, :]

        def trig2(f, t):
            return trig[:, None, 4 + f:8:2, t].to_broadcast([P, D // 4, 2])

        x_view = x.rearrange("(t r) s d -> (r s) t d", r=BT)
        out_view = out.rearrange("(t r) s d -> (r s) t d", r=BT)

        @block.sync
        def _(sp):
            sp.dma_start(dom_i[:, :], col(idx_domain)).then_inc(ld_dom, 16)
            for h in range(2):
                sp.dma_start(x_tok[:, h * HALF:(h + 1) * HALF, :],
                             x_view[:, h * HALF:(h + 1) * HALF, :]).then_inc(ld_x[h], 16)
            sp.dma_start(exp_i[:, :], everywhere(idx_expert, B)).then_inc(ld_exp, 16)
            sp.dma_start(expcol_i[:, :], col(idx_expert)).then_inc(ld_exp, 16)
            sp.dma_start(down_col[:, :], col(down_b)).then_inc(ld_dcol, 16)
            sp.dma_start(upT[A:A + 1, :], row(up_b)).then_inc(ld_upb, 16)
            for i, v in enumerate((theta, phi)):
                sp.dma_start(bat[:, i, :], everywhere(v, P)).then_inc(ld_bat, 16)
            sp.dma_start(bat_i[:, :], everywhere(idx_cond, P)).then_inc(ld_cond, 16)

            def load_wo(h):
                es = slice(h * E1 // 2, (h + 1) * E1 // 2)
                sp.dma_start(wo[:, es, :, :], Wo[es].rearrange("e (c i) h -> i e c h", i=P)).then_inc(ld_wo, 16)

            for n, (r0, v) in enumerate((
                    (R_G0, row(g0)), (R_BE0, row(be0)), (R_BI, bi.rearrange("e (c i) -> (e c) i", i=P)),
                    (R_BO, bo), (R_G1, g1), (R_BE1, be1), (R_NR, row(b1_nr)), (R_TSR, row(b1_tsr)),
                    (R_SR, b1_sr.rearrange("(a b) -> a b", b=P)), (R_SR2, row(b2_sr)),
                    (R_LAST, row(b2_nr)), (R_LAST + 1, row(b2_tsr)), (R_LAST + 2, row(b3_sr)))):
                if n in (2, 4):
                    load_wo(n // 2 - 1)
                sp.dma_start(vec_rows[r0:r0 + v.shape[0], :], v).then_inc(ld_vec, 16)

            def load_wi(e, k):
                sp.dma_start(wi_st[:, k, :],
                             Wi.rearrange("e h i -> (e h) i")[bass.ds(e * P, P), :]).then_inc(ld_wi[k], 16)

            sp.wait_ge(ld_win, 16)
            for w in range(3):
                load_wi(window_expert(ENG.SP, w), w)
            for k, v in ((0, w1_nr), (1, w1_tsr)):
                sp.dma_start(w1[:, k, :], v).then_inc(ld_l2, 16)
            sp.dma_start(w1[:, 2:4, :], w1_sr.rearrange("h (c k) -> h c k", k=P)).then_inc(ld_l2, 16)
            e = window_expert(ENG.SP, 3)
            sp.wait_ge(up_done, 2)
            load_wi(e, 0)
            sp.dma_start(w2s[:, :, :], w2_sr.rearrange("(c h) k -> h c k", h=P)).then_inc(ld_l2, 16)
            for k, v in enumerate((w2_nr, w2_tsr, w3_sr)):
                sp.dma_start(w_last[:, k, :], v).then_inc(ld_l2, 16)
            e = window_expert(ENG.SP, 4)
            sp.wait_ge(up_done, 4)
            load_wi(e, 1)
            for dst, v in ((g2r, g2), (be2r, be2)):
                sp.dma_start(dst[:, :], everywhere(v, P)).then_inc(ld_rows, 16)
            with sp.Fori(0, (NW - 5) // 3) as i:
                for k in range(3):
                    e = window_expert(ENG.SP, i * 3 + (5 + k))
                    sp.wait_ge(up_done, i * 6 + 2 * (3 + k))
                    load_wi(e, (5 + k) % 3)
            for t in range(0, NT, 2):
                if t in GROUPS_2[POOL_SUM]:
                    sp.wait_ge(y_pool_ready, 2)
                else:
                    sp.wait_ge(y_ready, t + 2 - (2 if t > GROUPS_2[POOL_SUM][0] else 0))
                sp.dma_start(out_view[:, t:t + 2, :], y[:, t:t + 2, :]).then_inc(stored, 16)
            sp.wait_ge(stored, 16 * NT // 2)

        @block.tensor
        def _(pe):
            T = nc.tensor
            pe.wait_ge(ident_ready, 1)

            def keep_warm(n, b):
                for _ in range(n):
                    T.matmul(bank[b][:, 0:P], ident[:, :], ident[:, :], start=True, stop=True)

            keep_warm(WARM_UP, 5)
            for h in range(2):
                pe.wait_ge(ld_x[h], 16)
                for k in range(HALF):
                    last = T.transpose(bank[h][:, k * P:(k + 1) * P], x_tok[:, h * HALF + k, :], ident[:, :])
                last.then_inc(xT_psum, 1)
                if h == 0:
                    pe.wait_ge(ld_du, 32)
                    T.transpose(bank[6][:, 0:A], down_rows[:, :], ident[0:A, 0:A])
                    T.transpose(bank[6][0:A, P:2 * P], up_rows[:, :], ident[:, :]).then_inc(small_psum, 1)
            pe.wait_ge(before_ready, 1)
            T.matmul(bank[7][0:B, 0:B + E1 + 1], ones[:, :], before[:, :], start=True, stop=True).then_inc(rank_psum, 1)
            pe.wait_ge(small_ready, 1)
            for h in range(2):
                pe.wait_ge(xT_ready, h + 1)
                T.matmul(bank[2 + h][0:A, :], downT[:, :], xT[:, h * HC:(h + 1) * HC],
                         start=True, stop=True).then_inc(hid_psum, 1)
            keep_warm(GELU_WAIT, 5)
            pe.wait_ge(wgT_ready, 1)
            for h in range(2):
                pe.wait_ge(hid_ready, h + 1)
                for k in range(HB):
                    b = h * HB + k
                    last = T.matmul(bank[4 + h][0:A, k * S:(k + 1) * S], wgT[:, :, b], hid[:, b * S:(b + 1) * S],
                                    start=True, stop=True)
                last.then_inc(hid2_psum, 1)
            keep_warm(BIAS_WAIT, 1)
            pe.wait_ge(up_ready, 1)
            pe.wait_ge(center_ready, 1)
            for h in range(2):
                pe.wait_ge(hid2_ready, h + 1)
                for k in range(HALF):
                    t = h * HALF + k
                    o = tile0(t)
                    T.matmul(o, xT[:, t * P:(t + 1) * P], center[:, :], start=True, stop=False)
                    last = T.matmul(o, hid2[:, t * P:(t + 1) * P], upT_c[:, :], start=False, stop=True)
                    if any(t == group[-1] for group in GROUPS_0):
                        last.then_inc(o0_psum, 1)
            pe.wait_ge(ld_vec, 16 * 13)
            T.transpose(bank[6][:, 2 * P:2 * P + NR], vec_rows[:, :],
                        ident[0:NR, 0:NR]).then_inc(small_psum, 1)
            for g, group in enumerate(GROUPS_0):
                if Z0T_BANK[g] == 6:
                    pe.wait_ge(small_ready, 3)
                pe.wait_ge(z0_ready, g + 1)
                for t in group:
                    last = T.transpose(z0T(t), z0[:, t, :], ident[:, :])
                last.then_inc(z0T_psum, 1)
                keep_warm(L0_WAITS[g], L0_BANK[g])

            def up(w):
                pe.wait_ge(ld_wi[w % 3], 16 * (w // 3 + 1))
                pe.wait_ge(xs_ready, w + 1)
                if w == 0:
                    pe.wait_ge(xs0_ready, 1)
                if w >= 2:
                    pe.wait_ge(gelu_done, 2 * (w - 1))
                for c in range(NC1):
                    last = T.matmul(up_chunk(w, c), wi_st[:, w % 3, c * P:(c + 1) * P],
                                    xs[:, w % NXS, :], start=True, stop=True)
                    if c % 2:
                        last.then_inc(up_done, 1)

            def down(w, e):
                pe.wait_ge(xr_ready, w + 1)
                if w >= 2:
                    pe.wait_ge(z1_ready, w - 1)
                o = bank[6 + w % 2][:, 0:D]
                T.matmul(o, xrT[:, w % 2, :], ident[:, :], start=True, stop=False, is_transpose=True)
                for c in range(NC1):
                    pe.wait_ge(gelu_done, 2 * w + c // 2 + 1)
                    last = T.matmul(o, hT[:, w % 2, c * P:(c + 1) * P], wo[:, bass.ds(e, 1), c, :],
                                    start=False, stop=(c == NC1 - 1))
                last.then_inc(down_done, 1)

            def backT(w):
                pe.wait_ge(z1_ready, w + 1)
                if w >= 2:
                    pe.wait_ge(x2_act if w % 2 else x2_dve, scattered(w - 2, w % 2))
                for n in range(2):
                    if slots(w, n):
                        rows = slice(slots(w, n)[0] * S, (slots(w, n)[-1] + 1) * S)
                        last = T.transpose(z1T(w, n, slots(w, n)), z1[rows, w % LAG, :], ident[rows, rows])
                last.then_inc(z1T_done, 1)

            pe.wait_ge(ld_win, 16)
            for w in range(NW + LAG):
                if w < NW:
                    e_next = window_expert(ENG.PE, w)
                    up(w)
                if w == NW:
                    backT(w - LAG)
                if 1 <= w <= NW:
                    if w == 1:
                        pe.wait_ge(ld_wo, 32)
                    down(w - 1, e_now)
                e_now = e_next
                if w >= LAG and w != NW:
                    backT(w - LAG)
                if w >= NW:
                    keep_warm(L1_WAITS[w - NW], 2)

            pe.wait_ge(x2_dve, scattered(NW - 1, 0))
            pe.wait_ge(x2_act, scattered(NW - 1, 1))
            pe.wait_ge(ld_l2, 16 * 7)

            def first_layer(h, k):
                T.matmul(bank[L2_BANK[h, k]][:, :], w1[:, k, :], x2T[:, h * HC:(h + 1) * HC],
                         start=True, stop=True).then_inc(l2_psum, 1)

            def second_layer(h):
                b = bank[L2_BANK[h, 4]][:, :]
                T.matmul(b, w2s[:, 0, :], h2[:, h, 2, :], start=True, stop=False)
                T.matmul(b, w2s[:, 1, :], h2[:, h, 3, :], start=False, stop=True).then_inc(l2_psum, 1)

            def last_layer(g):
                h = GROUPS_2[g][0] // HALF
                pe.wait_ge(x2r_ready, 2)
                pe.wait_ge(masked_01, 2 * h + 2)
                pe.wait_ge(masked_2, h + 1)
                pe.wait_ge(w_last_ready, 1)
                for t in GROUPS_2[g]:
                    c = slice((t % HALF) * P, (t % HALF + 1) * P)
                    T.matmul(tile2(t), x2rT[:, t * P:(t + 1) * P], center[:, :], start=True, stop=False)
                    T.matmul(tile2(t), h2[:, h, 0, c], w_last_c[:, 0, :], start=False, stop=False)
                    T.matmul(tile2(t), h2[:, h, 1, c], w_last_c[:, 1, :], start=False, stop=False)
                    last = T.matmul(tile2(t), h3[:, h, c], w_last_c[:, 2, :], start=False, stop=True)
                last.then_inc(last_psum, 1)

            for h, k in L2_ORDER[:6]:
                first_layer(h, k)
            pe.wait_ge(l2_gelu, 4)
            second_layer(0)
            first_layer(1, 2)
            first_layer(1, 3)
            last_layer(0)
            pe.wait_ge(l2_gelu, 9)
            second_layer(1)
            for g in range(1, len(GROUPS_2)):
                last_layer(g)

        @block.scalar
        def _(act):
            V = nc.scalar
            act.dma_start(down_rows[:, :], down_W).then_inc(ld_du, 16)
            act.dma_start(up_rows[:, :], up_W).then_inc(ld_du, 16)
            act.wait_ge(warm_ready, 1)
            V.activation(warm[:, 0:1], warm[:, 3:4], ACT.Gelu)
            for h in range(2):
                act.wait_ge(xT_psum, h + 1)
                V.copy(xT[:, h * HC:(h + 1) * HC], bank[h][:, :]).then_inc(xT_ready, 1)
                if h == 0:
                    act.wait_ge(small_psum, 1)
                    V.copy(downT[:, :], bank[6][:, 0:A]).then_inc(small_ready, 1)
            V.copy(upT[0:A, :], bank[6][0:A, P:2 * P]).then_inc(small_ready, 1)
            act.wait_ge(small_ready, 2)
            act.wait_ge(ld_upb, 16)
            V.activation(squares[0:A + 1, 0, :], upT[:, :], ACT.Copy, accum_out=up_sum[:, :]).then_inc(up_sum_ready, 1)
            act.wait_ge(ld_dcol, 16)
            for h in range(2):
                act.wait_ge(hid_psum, h + 1)
                V.activation(hid[:, h * HC:(h + 1) * HC], bank[2 + h][0:A, :], ACT.Gelu,
                             bias=down_col[:, 0:1]).then_inc(hid_ready, 1)
            V.activation(warm[:, 1:2], warm[:, 3:4], ACT.Sin)
            act.wait_ge(angles_ready, 1)
            V.activation(trig[:, 0:4, :].rearrange("p (n f) t -> p n f t", f=2),
                         ang[:, 0:2, None, :].to_broadcast([P, 2, 2, NT]), ACT.Sin)
            V.activation(trig[:, 4:8:2, :], ang[:, 2:4, :], ACT.Sin)
            V.activation(trig[:, 5:8:2, :], ang[:, 2:4, :], ACT.Sin, scale=-1.0).then_inc(trig_ready, 1)
            V.activation(warm[:, 2:3], warm[:, 3:4], ACT.Gelu)

            def sum_squares(group, tile):
                for t in group:
                    last = V.activation(squares[:, t, :], tile(t), ACT.Square, accum_out=sumsq[:, t:t + 1])
                last.then_inc(sumsq_ready, 1)

            for g, group in enumerate(GROUPS_0):
                act.wait_ge(o0_psum, g + 1)
                sum_squares(group, tile0)
                if g == 1:
                    act.wait_ge(win_ready, 1)
                    act.dma_start(win.rearrange("a (w n) -> a w n", n=WROW), win_p[0:NW, :]).then_inc(ld_win, 16)
            act.wait_ge(small_psum, 2)
            V.copy(vecT[:, :], bank[6][:, 2 * P:2 * P + NR]).then_inc(small_ready, 1)
            act.wait_ge(small_ready, 3)
            for g, group in enumerate(GROUPS_0):
                act.wait_ge(z0T_psum, g + 1)
                V.activation(x1T[:, group[0] * P:(group[-1] + 1) * P], bank[Z0T_BANK[g]][:, 0:len(group) * P],
                             ACT.Identity, bias=vecT[:, R_BE0:R_BE0 + 1],
                             scale=vecT[:, R_G0:R_G0 + 1]).then_inc(x1_ready, 1)
            act.wait_ge(ld_win, 16)

            def old_registers(v):
                return window_expert(ENG.Activation, v), window_columns(ENG.Activation, v, slots(v, 1))

            def scatter(v, e, cols):
                act.wait_ge(z1T_done, v + 1)
                for j, c in zip(slots(v, 1), cols):
                    last = V.activation(x2T[:, bass.ds(c, S)], z1T(v, 1, [j]), ACT.Identity,
                                        bias=vecT[:, bass.ds(e + R_BE1, 1)], scale=vecT[:, bass.ds(e + R_G1, 1)])
                last.then_inc(x2_act, 1)

            for w in range(NW):
                v = w - LAG
                if v >= 0 and slots(v, 1):
                    old = old_registers(v)
                e = window_expert(ENG.Activation, w)
                if w >= 2:
                    act.wait_ge(down_done, w - 1)
                for c in range(NC1):
                    act.wait_ge(up_done, 2 * w + c // 2 + 1)
                    last = V.activation(hT[:, w % 2, c * P:(c + 1) * P], up_chunk(w, c), ACT.Gelu,
                                        bias=vecT[:, bass.ds(e * NC1 + (R_BI + c), 1)])
                    if c % 2:
                        last.then_inc(gelu_done, 1)
                if v >= 0 and slots(v, 1):
                    scatter(v, *old)
            rest = [(v, *old_registers(v)) for v in range(NW - LAG, NW) if slots(v, 1)]
            for v, e, cols in rest:
                scatter(v, e, cols)

            def l2_gelu_of(n):
                h, k = L2_ORDER[n]
                act.wait_ge(l2_psum, n + 1)
                dst = h3[:, h, :] if k == 4 else h2[:, h, k, :]
                r = (R_NR, R_TSR, R_SR, R_SR + 1, R_SR2)[k]
                V.activation(dst, bank[L2_BANK[h, k]][:, :], ACT.Gelu, bias=vecT[:, r:r + 1]).then_inc(l2_gelu, 1)

            def l2_squares(g):
                act.wait_ge(last_psum, g + 1)
                sum_squares(GROUPS_2[g], tile2)

            def l2_cosines(g):
                for t in GROUPS_2[g]:
                    act.wait_ge(z2_ready, t + 1)
                    for a in range(2):
                        last = V.activation(pairs(y_a, t)[:, :, a, :], pairs(z2, t)[:, :, a, :], ACT.Copy,
                                            scale=trig[:, 2 * a, t:t + 1])
                    last.then_inc(ya_ready, 1)

            for n in range(len(L2_ORDER) - 1):
                l2_gelu_of(n)
            l2_squares(0)
            l2_gelu_of(len(L2_ORDER) - 1)
            l2_cosines(0)
            l2_squares(1)
            l2_squares(2)
            l2_cosines(1)
            l2_squares(3)
            l2_squares(4)
            l2_cosines(2)
            l2_cosines(3)

        @block.vector
        def _(dve):
            V = nc.vector
            steps = [0]

            def then(ins):
                steps[0] += 1
                ins.then_inc(dstep, 1)
                dve.wait_ge(dstep, steps[0])

            def step(ins):
                steps[0] += 1
                ins.then_inc(dstep, 1)
                return steps[0]

            def after(number):
                dve.wait_ge(dstep, number)

            V.memset(ones[:, :], 1.0)
            V.memset(hid2[A:A + 1, :], 1.0)
            V.memset(win_p[:, :], 0)
            dve.wait_ge(ld_dom, 16)
            then(V.tensor_copy(dom[:, 0:1], dom_i[:, :]))
            then(V.tensor_scalar(dom[:, 1:2], dom[:, 0:1], 0.0, float(E0 - 1), ALU.max, ALU.min))
            V.tensor_copy(dom_idx[:, :], dom[:, 1:2]).then_inc(idx_ready, 1)
            then(V.tensor_tensor(dom[:, 2:3], dom[:, 0:1], dom[:, 1:2], ALU.is_equal))
            V.tensor_scalar(dom[:, 3:4], dom[:, 2:3], -1.0, 1.0, ALU.mult, ALU.add)
            V.memset(x1T[:, PAD:], 0.0)
            dve.wait_ge(ld_exp, 32)
            dve.wait_ge(consts, 1)
            V.tensor_copy(exp_f[:, :], exp_i[:, :])
            then(V.tensor_copy(keycol[:, 0:1], expcol_i[:, :]))
            V.scalar_tensor_tensor(keys[:, :], exp_f[:, :], float(B), iota_r[:, :], ALU.mult, ALU.add)
            then(V.scalar_tensor_tensor(keycol[:, 1:2], keycol[:, 0:1], float(B), iota_p[:, :], ALU.mult, ALU.add))
            V.tensor_scalar(before[:, 0:B], keys[:, :], keycol[:, 1:2], None, ALU.is_gt)
            V.tensor_scalar(before[:, B:], iota_r[:, 0:E1 + 1], keycol[:, 0:1], None, ALU.is_gt
                            ).then_inc(before_ready, 1)

            rank, s_cum = bank[7][0:B, 0:B], bank[7][0:B, B:B + E1 + 1]
            dve.wait_ge(ld_wg, 16)
            scaled = step(V.tensor_scalar(wg[:, :, :], wg[:, :, :], dom[:, 2:3], None, ALU.mult))
            dve.wait_ge(rank_psum, 1)
            n = step(V.tensor_scalar(first[:, :], s_cum, win_place[:, 0:1], None, ALU.add))
            after(n)
            n = step(V.tensor_tensor(n_e[:, :], first[:, 1:E1 + 1], first[:, 0:E1], ALU.subtract))
            diagonal = wg.rearrange("b o a -> b (o a)")[:, ::A + 1]
            after(scaled)
            unit = step(V.tensor_scalar(diagonal, diagonal, dom[:, 3:4], None, ALU.add))
            after(n)
            n = step(V.scalar_tensor_tensor(c_nw[:, :, :], iota_r[:, None, 0:E1].to_broadcast([B, E1, E1]), float(BT),
                                            n_e[:, :, None].to_broadcast([B, E1, E1]), ALU.mult, ALU.is_lt))
            n_less = step(V.tensor_scalar(n_left[:, :], n_e[:, :], win_place[:, 0:1], None, ALU.subtract))
            after(unit)
            V.transpose(wgT.rearrange("a o b -> a (o b)"), wg.rearrange("b o a -> b (o a)")).then_inc(wgT_ready, 1)
            after(n)
            n = step(V.tensor_reduce(nw_e[:, :], c_nw[:, :, :], AX.X, ALU.add))
            dve.wait_ge(ld_eb, 32)
            bias = step(V.scalar_tensor_tensor(bsum[:, :], eb_rows[:, :], dom[:, 2:3], emb_rows[:, :],
                                               ALU.mult, ALU.add))
            after(n)
            n = step(V.tensor_tensor(c_tri[:, :, :], tri[:, :, :], nw_e[:, None, :].to_broadcast([B, E1, E1]),
                                     ALU.mult))
            after(bias)
            bias = step(V.transpose(bsumT[:, :], bsum[:, :]))
            dve.wait_ge(up_sum_ready, 1)
            mean = step(V.tensor_scalar(up_mean[:, :], up_sum[:, :], -1.0 / D, None, ALU.mult))
            after(n)
            then(V.tensor_reduce(cw[:, :], c_tri[:, :, :], AX.X, ALU.add))
            after(mean)
            V.tensor_scalar(upT_c[:, :], upT[:, :], up_mean[:, 0:1], None, ALU.add).then_inc(up_ready, 1)
            V.tensor_scalar(c_w[:, :], cw[:, :], iota_p[:, 0:1], None, ALU.is_le)
            n = step(V.tensor_tensor(cwx[:, :], cw[:, :], nw_e[:, :], ALU.subtract))

            def add_bias(h):
                dve.wait_ge(hid2_psum, h + 1)
                V.tensor_tensor(hid2[0:A, h * HC:(h + 1) * HC].rearrange("o (b s) -> o b s", s=S),
                                bank[4 + h][0:A, :].rearrange("o (b s) -> o b s", s=S),
                                bsumT[:, h * HB:(h + 1) * HB, None].to_broadcast([A, HB, S]),
                                ALU.add).then_inc(hid2_ready, 1)

            after(n)
            after(n_less)
            V.tensor_reduce(wv[:, 0:1], c_w[:, :], AX.X, ALU.add)
            V.scalar_tensor_tensor(by_e[:, 0, :], cwx[:, :], -float(BT), first[:, 0:E1], ALU.mult, ALU.add)
            then(V.scalar_tensor_tensor(by_e[:, 1, :], cwx[:, :], float(BT), n_left[:, :], ALU.mult, ALU.add))
            V.tensor_scalar(win_p[:, BT:BT + 1], wv[:, 0:1], float(E1 - 1), None, ALU.min)
            n = step(V.scalar_tensor_tensor(c_s[:, :, :], iota_r[:, None, 0:E1].to_broadcast([B, 2, E1]), wv[:, 0:1],
                                        by_e[:, :, :], ALU.is_equal, ALU.mult))
            after(bias)
            add_bias(0)
            after(n)
            then(V.tensor_reduce(wv[:, 1:3], c_s[:, :, :], AX.X, ALU.add))
            V.tensor_scalar(taken[:, :], place_32[:, :], wv[:, 2:3], None, ALU.is_lt)
            n = step(V.tensor_scalar(places[:, :], place_32[:, :], wv[:, 1:2], None, ALU.add))
            add_bias(1)
            after(n)
            dve.wait_ge(late_consts, 1)
            for j in range(BT):
                last = V.scalar_tensor_tensor(c_slot[:, j, :], rank, places[:, j:j + 1], col_less_pad[:, j, :],
                                              ALU.is_equal, ALU.mult)
            then(last)
            then(V.tensor_reduce(slot[:, :], c_slot[:, :, :], AX.X, ALU.add))
            then(V.tensor_tensor(slot[:, :], slot[:, :], taken[:, :], ALU.mult))
            V.tensor_tensor(win_p[:, 0:BT], slot[:, :], pad_col[:, :], ALU.add).then_inc(win_ready, 1)

            for g, group in enumerate(GROUPS_0):
                dve.wait_ge(o0_psum, g + 1)
                dve.wait_ge(rstd_ready, g + 1)
                for t in group:
                    last = V.tensor_scalar(z0[:, t, :], tile0(t), rstd[:, t:t + 1], None, ALU.mult)
                last.then_inc(z0_ready, 1)

            def last_biases():
                dve.wait_ge(ld_cond, 16)
                then(V.tensor_copy(cond[:, :], bat_i[:, :]))
                for c in range(3):
                    last = V.tensor_scalar(holds[:, c, :], cond[:, :], float(c), None, ALU.is_equal)
                then(last)
                then(V.tensor_scalar(last_b[:, :], holds[:, 0, :], vecT[:, R_LAST:R_LAST + 1], None, ALU.mult))
                for c in (1, 2):
                    ins = V.scalar_tensor_tensor(last_b[:, :], holds[:, c, :], vecT[:, R_LAST + c:R_LAST + c + 1],
                                                 last_b[:, :], ALU.mult, ALU.add)
                    if c == 1:
                        then(ins)
                ins.then_inc(last_b_ready, 1)

            dve.wait_ge(small_ready, 3)

            def residual(w, e):
                dve.wait_ge(xs_ready, w + 1)
                if w == 0:
                    dve.wait_ge(xs0_ready, 1)
                if w >= 2:
                    dve.wait_ge(down_done, w - 1)
                V.tensor_scalar(xrT[:, w % 2, :], xs[:, w % NXS, :], vecT[:, bass.ds(e + R_BO, 1)], None,
                                ALU.add).then_inc(xr_ready, 1)

            def norm_stats(w):
                dve.wait_ge(down_done, w + 1)
                then(V.bn_stats(st1[:, w % 2, :], bank[6 + w % 2][:, 0:D]))
                V.bn_aggr(mv1[:, w % 2, :], st1[:, w % 2, :]).then_inc(mv1_ready, 1)

            def normalize(w):
                dve.wait_ge(mv1_ready, w + 1)
                dve.wait_ge(rstd1_ready, w + 1)
                if w >= LAG:
                    dve.wait_ge(z1T_done, w - LAG + 1)
                V.tensor_scalar(z1[:, w % LAG, :], bank[6 + w % 2][:, 0:D], mv1[:, w % 2, 0:1],
                                rstd1[:, w % 2, 0:1], ALU.subtract, ALU.mult).then_inc(z1_ready, 1)

            def scatter(w, e, cols):
                dve.wait_ge(z1T_done, w + 1)
                for j, c in zip(slots(w, 0), cols):
                    last = V.tensor_scalar(x2T[:, bass.ds(c, S)], z1T(w, 0, [j]),
                                           vecT[:, bass.ds(e + R_G1, 1)], vecT[:, bass.ds(e + R_BE1, 1)],
                                           ALU.mult, ALU.add)
                last.then_inc(x2_dve, 1)

            dve.wait_ge(ld_win, 16)
            rest = range(BT // 2, BT)
            cols = window_columns(ENG.DVE, 0, rest)
            e_next = window_expert(ENG.DVE, 0)
            dve.wait_ge(x1_ready, len(GROUPS_0))
            for j, c in zip(rest, cols):
                last = V.tensor_copy(xs[:, 0, j * S:(j + 1) * S], x1T[:, bass.ds(c, S)])
            last.then_inc(xs0_ready, 1)
            for w in range(NW):
                residual(w, e_next)
                if w == 0:
                    last_biases()
                if w >= 1:
                    norm_stats(w - 1)
                if w >= LAG and slots(w - LAG, 0):
                    scatter(w - LAG, e_old, cols)
                if w + 1 < NW:
                    e_next = window_expert(ENG.DVE, w + 1)
                v = w + 1 - LAG if w < NW - 1 else NW - 2
                if v >= 0 and slots(v, 0):
                    e_old, cols = window_expert(ENG.DVE, v), window_columns(ENG.DVE, v, slots(v, 0))
                if 1 <= w < NW - 1:
                    normalize(w - 1)
            norm_stats(NW - 1)
            normalize(NW - 2)
            e_last, cols_last = window_expert(ENG.DVE, NW - 1), window_columns(ENG.DVE, NW - 1, slots(NW - 1, 0))
            normalize(NW - 1)
            scatter(NW - 2, e_old, cols)
            scatter(NW - 1, e_last, cols_last)

            def mask_2(h):
                dve.wait_ge(l2_gelu, (7, 10)[h])
                t3 = h3[:, h, :].rearrange("p (b s) -> p b s", s=S)
                V.tensor_tensor(t3, t3, holds[:, 2, h * HB:(h + 1) * HB, None].to_broadcast([P, HB, S]),
                                ALU.mult).then_inc(masked_2, 1)

            def l2_gamma(g):
                dve.wait_ge(last_psum, g + 1)
                dve.wait_ge(sumsq_ready, len(GROUPS_0) + g + 1)
                dve.wait_ge(ld_rows, 32)
                for t in GROUPS_2[g]:
                    last = V.tensor_tensor(u2[:, t, :], tile2(t), g2r[:, :], ALU.mult)
                return step(last)

            def l2_beta(g, gamma):
                dve.wait_ge(rstd_ready, len(GROUPS_0) + g + 1)
                after(gamma)
                for t in GROUPS_2[g]:
                    V.scalar_tensor_tensor(z2[:, t, :], u2[:, t, :], rstd[:, t:t + 1], be2r[:, :],
                                           ALU.mult, ALU.add).then_inc(z2_ready, 1)

            def l2_sines(g):
                last = None
                dve.wait_ge(trig_ready, 1)
                for t in GROUPS_2[g]:
                    if t != POOL_SINES:
                        dve.wait_ge(z2_ready, t + 1)
                        for f in range(2):
                            last = V.tensor_tensor(pairs(y_b, t)[:, :, :, f], pairs(z2, t)[:, :, :, 1 - f],
                                                   trig2(f, t), ALU.mult)
                    if t == NT - 1:
                        last = V.tensor_tensor(fours(y_a, t), fours(z2, t), trig4(0, t), ALU.mult)
                if g == POOL_SUM:
                    last.then_inc(yb_dve_ready, 1)
                    return None
                return step(last)

            def l2_sum(g, sines):
                for t in GROUPS_2[g]:
                    if t < NT - 1:
                        dve.wait_ge(ya_ready, t + 1)
                    if t == POOL_SINES:
                        dve.wait_ge(yb_ready, 1)
                    else:
                        after(sines)
                    V.tensor_tensor(y[:, t, :], y_a[:, t, :], y_b[:, t, :], ALU.add).then_inc(y_ready, 1)

            for h in range(2):
                dve.wait_ge(last_b_ready, 1)
                dve.wait_ge(x2_dve, scattered(NW - 1, 0))
                dve.wait_ge(x2_act, scattered(NW - 1, 1))
                V.tensor_tensor(x2rT[:, h * HC:(h + 1) * HC].rearrange("p (b s) -> p b s", s=S),
                                x2T[:, h * HC:(h + 1) * HC].rearrange("p (b s) -> p b s", s=S),
                                last_b[:, h * HB:(h + 1) * HB, None].to_broadcast([P, HB, S]),
                                ALU.add).then_inc(x2r_ready, 1)
            dve.wait_ge(ld_l2, 16 * 7)
            then(V.tensor_reduce(w_sum[:, :], w_last[:, :, :], AX.X, ALU.add))
            then(V.tensor_scalar(w_mean[:, :], w_sum[:, :], -1.0 / D, None, ALU.mult))
            V.tensor_tensor(w_last_c[:, :, :], w_last[:, :, :], w_mean[:, :, None].to_broadcast([P, 3, D]),
                            ALU.add).then_inc(w_last_ready, 1)
            mask_2(0)
            gamma, sines = {0: l2_gamma(0)}, {}
            for g in range(3):
                l2_beta(g, gamma[g])
                if g == 0:
                    mask_2(1)
                sines[g] = l2_sines(g)
                gamma[g + 1] = l2_gamma(g + 1)
                if g == 1:
                    l2_sum(0, sines[0])
            gamma[4] = l2_gamma(4)
            l2_sum(1, sines[1])
            for g in (3, 4):
                l2_beta(g, gamma[g])
            for g in (3, 4):
                sines[g] = l2_sines(g)
            for g in (3, 4):
                l2_sum(g, sines[g])

        @block.gpsimd
        def _(pool):
            V = nc.gpsimd
            steps = [0]

            def then(ins):
                steps[0] += 1
                ins.then_inc(pstep, 1)
                pool.wait_ge(pstep, steps[0])

            V.memset(warm[:, 3:4], 0.0).then_inc(warm_ready, 1)
            then(V.memset(ident[:, :], 0.0))
            V.affine_select(ident[:, :], ident[:, :], [[1, P]], ALU.not_equal, 1.0, base=0,
                            channel_multiplier=-1).then_inc(ident_ready, 1)
            V.memset(quad[:, :], 1.0)
            V.memset(mhalf[:, :], -0.5)
            V.memset(tri[:, :, :], 1.0)
            V.iota(iota_r[:, :], [[1, B]], base=0, channel_multiplier=0, allow_small_or_imprecise_dtypes=True)
            V.iota(iota_p[:, :], [[0, 1]], base=0, channel_multiplier=1, allow_small_or_imprecise_dtypes=True)
            V.iota(place_32[:, :], [[1, BT]], base=B, channel_multiplier=0, allow_small_or_imprecise_dtypes=True)
            then(V.iota(win_place[:, :], [[0, 1]], base=-B, channel_multiplier=BT,
                        allow_small_or_imprecise_dtypes=True))
            V.affine_select(tri[:, :, :], tri[:, :, :], [[1, E1], [-1, E1]], ALU.is_ge, 0.0, base=0,
                            channel_multiplier=0).then_inc(consts, 1)
            pool.wait_ge(idx_ready, 1)
            for dst, src, done in ((wg.rearrange("b o a -> b (o a)"), expert_W.rearrange("e o a -> e (o a)"), ld_wg),
                                   (eb_rows, expert_b, ld_eb), (emb_rows, domain_emb, ld_eb)):
                pool.indirect_dma_start(out=dst[:, :], out_offset=None, in_=src,
                                        in_offset=bass.IndirectOffsetOnAxis(ap=dom_idx[:, 0:1], axis=0)
                                        ).then_inc(done, 16)
            V.iota(pad_col[:, :], [[S, BT]], base=PAD, channel_multiplier=BT * S, allow_small_or_imprecise_dtypes=True)
            V.iota(col_less_pad[:, :, :], [[-S, BT], [S, B]], base=-PAD, channel_multiplier=-BT * S,
                   allow_small_or_imprecise_dtypes=True)
            then(V.affine_select(quad[:, :], quad[:, :], [[-S, BT]], ALU.is_ge, 0.0, base=0, channel_multiplier=1))
            V.affine_select(quad[:, :], quad[:, :], [[S, BT]], ALU.is_ge, 0.0, base=S - 1,
                            channel_multiplier=-1).then_inc(late_consts, 1)

            pool.wait_ge(ld_bat, 32)
            pool.wait_ge(late_consts, 1)
            then(V.tensor_tensor(ang_q[:, :, :], bat[:, :, :].rearrange("p n (t r) -> p (n t) r", r=BT),
                                 quad[:, None, :].to_broadcast([P, 2 * NT, BT]), ALU.mult))
            then(V.tensor_tensor(ang_q[:, :, 0:2], ang_q[:, :, 0:2], ang_q[:, :, 2:4], ALU.add))
            then(V.tensor_tensor(ang[:, 2:4, :].rearrange("p n t -> p (n t)"), ang_q[:, :, 0], ang_q[:, :, 1], ALU.add))
            then(V.tensor_scalar(ang[:, 0:2, :], ang[:, 2:4, :], -1.0, HALF_PI, ALU.mult, ALU.add))
            then(V.tensor_scalar(turns[:, :, :], ang[:, :, :], 1 / (4 * HALF_PI), ROUND, ALU.mult, ALU.add))
            then(V.tensor_scalar(turns[:, :, :], turns[:, :, :], ROUND, None, ALU.subtract))
            for n, part in enumerate((TWO_PI_HIGH, TWO_PI_LOW)):
                then(V.tensor_scalar(whole[:, :, :], turns[:, :, :], -part, None, ALU.mult))
                last = V.tensor_tensor(ang[:, :, :], ang[:, :, :], whole[:, :, :], ALU.add)
                if n == 0:
                    then(last)
            last.then_inc(angles_ready, 1)
            V.tensor_scalar(center[:, :], ident[:, :], 1.0 / D, None, ALU.subtract).then_inc(center_ready, 1)

            def rstd_of(n, group, eps):
                pool.wait_ge(sumsq_ready, n + 1)
                ts = slice(group[0], group[-1] + 1)
                then(V.tensor_scalar(vpe[:, ts], sumsq[:, ts], 1.0 / D, eps, ALU.mult, ALU.add))
                V.tensor_tensor(rstd[:, ts], vpe[:, ts], mhalf[:, 0:len(group)], ALU.pow).then_inc(rstd_ready, 1)

            for g, group in enumerate(GROUPS_0):
                rstd_of(g, group, EPS0)

            pool.wait_ge(ld_win, 16)

            def gather(w):
                own = range(BT // 2 if w == 0 else BT)
                cols = window_columns(ENG.Pool, w, own)
                if w == 0:
                    pool.wait_ge(x1_ready, len(GROUPS_0))
                if w >= NXS:
                    pool.wait_ge(up_done, 2 * (w - NXS + 1))
                    pool.wait_ge(xr_ready, w - NXS + 1)
                for j, c in zip(own, cols):
                    last = V.tensor_copy(xs[:, w % NXS, j * S:(j + 1) * S], x1T[:, bass.ds(c, S)])
                last.then_inc(xs_ready, 1)

            for w in range(NXS):
                gather(w)
            for w in range(NW):
                pool.wait_ge(mv1_ready, w + 1)
                then(V.tensor_scalar(vpe1[:, w % 2, :], mv1[:, w % 2, 1:2], EPS1, None, ALU.add))
                V.tensor_tensor(rstd1[:, w % 2, :], vpe1[:, w % 2, :], mhalf[:, 0:1], ALU.pow).then_inc(rstd1_ready, 1)
                if w + NXS < NW:
                    gather(w + NXS)

            pool.wait_ge(last_b_ready, 1)
            for h in range(2):
                for c in range(2):
                    pool.wait_ge(l2_gelu, (1, 5)[h] + c)
                    t3 = h2[:, h, c, :].rearrange("p (b s) -> p b s", s=S)
                    V.tensor_tensor(t3, t3, holds[:, c, h * HB:(h + 1) * HB, None].to_broadcast([P, HB, S]),
                                    ALU.mult).then_inc(masked_01, 1)
            pool.wait_ge(trig_ready, 1)
            for g, group in enumerate(GROUPS_2):
                rstd_of(len(GROUPS_0) + g, group, EPS2)
                if g == 0:
                    t = POOL_SINES
                    pool.wait_ge(z2_ready, t + 1)
                    for f in range(2):
                        last = V.tensor_tensor(pairs(y_b, t)[:, :, :, f], pairs(z2, t)[:, :, :, 1 - f],
                                               trig2(f, t), ALU.mult)
                    last.then_inc(yb_ready, 1)
            pool.wait_ge(yb_dve_ready, 1)
            for t in GROUPS_2[POOL_SUM]:
                pool.wait_ge(ya_ready, t + 1)
                V.tensor_tensor(y[:, t, :], y_a[:, t, :], y_b[:, t, :], ALU.add).then_inc(y_pool_ready, 1)


_INS = ['x', 'itok_B_0_15', 'itok_B_0_7', 'itok_B_0_2', 'condB_theta', 'condB_phi',
        'L0_cond_down_W', 'L0_cond_down_b', 'L0_cond_up_W', 'L0_cond_up_b', 'L0_cond_expert_W',
        'L0_cond_expert_b', 'L0_cond_domain_emb', 'L0_cond_ln_gamma', 'L0_cond_ln_beta',
        'L1_cond_Wi', 'L1_cond_bi', 'L1_cond_Wo', 'L1_cond_bo', 'L1_cond_gamma', 'L1_cond_beta',
        'L2_cond_w1_nr', 'L2_cond_b1_nr', 'L2_cond_w2_nr', 'L2_cond_b2_nr',
        'L2_cond_w1_tsr', 'L2_cond_b1_tsr', 'L2_cond_w2_tsr', 'L2_cond_b2_tsr',
        'L2_cond_w1_sr', 'L2_cond_b1_sr', 'L2_cond_w2_sr', 'L2_cond_b2_sr', 'L2_cond_w3_sr', 'L2_cond_b3_sr',
        'L2_cond_gamma', 'L2_cond_beta']


def kernel(**inputs):
    import numpy as np
    import concourse.bacc as bacc
    from concourse.bass_utils import run_bass_kernel_spmd

    nc = bacc.Bacc("TRN2", target_bir_lowering=False, num_devices=1)
    arrays, args = {}, []
    for name in _INS:
        a = np.ascontiguousarray(inputs[name])
        arrays[f"in_{name}"] = a
        args.append(nc.dram_tensor(f"in_{name}", a.shape, mybir.dt.from_np(a.dtype), kind="ExternalInput").ap())
    out = nc.dram_tensor("out_x", (B, S, D), fp32, kind="ExternalOutput").ap()
    conditional_layers(nc, *args, out)
    return run_bass_kernel_spmd(nc, [arrays], core_ids=[0]).results[0]["out_x"]
```
